# Optimizing a Trainium2 kernel written in Bass

```python
import numpy as np
import jax
import jax.numpy as jnp

def _softmax(x, axis=-1):
    return jax.nn.softmax(x, axis=axis)

def _gelu(x):
    return jax.nn.gelu(x, approximate=True)

def _silu(x):
    return jax.nn.silu(x)

def _sigmoid(x):
    return jax.nn.sigmoid(x)

def _layernorm(x, axis=-1, eps=1e-05):
    m = jnp.mean(x, axis=axis, keepdims=True)
    v = jnp.var(x, axis=axis, keepdims=True)
    return (x - m) / jnp.sqrt(v + eps)

def _scatter_add(tgt, idx, src, axis=0):
    return tgt.at[idx].add(src)

def _segment_sum(src, seg, n):
    return jax.ops.segment_sum(src, seg, n)
kernel_name = 'mk_adj_preln_d1_adj_r2_1a02b4'

def setup_inputs(seed: int=0):
    np.random.seed(seed)
    _w = jnp.asarray

    def _rec_inputs():
        import jax
        import jax.numpy as jnp
        _gk = jax.random.key(seed)
        x = -0.0002928 + 1 * jax.random.normal(jax.random.fold_in(_gk, 1), (16, 512, 256), jnp.float32)
        _a = jax.random.bernoulli(jax.random.fold_in(_gk, 2), 0.03125, (512, 512))
        _a = jnp.logical_or(_a, jnp.swapaxes(_a, -1, -2))
        _a = jnp.logical_or(_a, jnp.eye(512, dtype=bool))
        _af = _a.astype(jnp.float32)
        adj = _af
        return (x, adj)
    x, adj = _rec_inputs()

    def _L0_gnn_setup():
        import jax, jax.numpy as jnp
        import numpy as np
        B, N, D, H = (4, 1024, 256, 8)
        HD = D // H
        key = jax.random.key(seed)
        ks = jax.random.split(key, 10)
        x = jax.random.normal(ks[0], (B, N, D), dtype=jnp.float32)
        adj = (jax.random.uniform(ks[1], (N, N)) < 0.1).astype(jnp.float32)
        s = 1.0 / np.sqrt(D)
        Wq = jax.random.normal(ks[2], (D, D), dtype=jnp.float32) * s
        Wk = jax.random.normal(ks[3], (D, D), dtype=jnp.float32) * s
        Wv = jax.random.normal(ks[4], (D, D), dtype=jnp.float32) * s
        Wo = jax.random.normal(ks[5], (D, D), dtype=jnp.float32) * s
        bq = jnp.zeros((D,), jnp.float32)
        bk = jnp.zeros((D,), jnp.float32)
        bv = jnp.zeros((D,), jnp.float32)
        bo = jnp.zeros((D,), jnp.float32)
        return {'x': x, 'adj': adj, 'Wq': Wq, 'bq': bq, 'Wk': Wk, 'bk': bk, 'Wv': Wv, 'bv': bv, 'Wo': Wo, 'bo': bo}
    _L0_gnn_all = _L0_gnn_setup()
    _L0_gnn_in = {k: v for k, v in _L0_gnn_all.items() if k in ('Wq', 'bq', 'Wk', 'bk', 'Wv', 'bv', 'Wo', 'bo')}
    del _L0_gnn_all
    return {'x': x, 'adj': adj, 'L0_gnn_Wq': _L0_gnn_in['Wq'], 'L0_gnn_bq': _L0_gnn_in['bq'], 'L0_gnn_Wk': _L0_gnn_in['Wk'], 'L0_gnn_bk': _L0_gnn_in['bk'], 'L0_gnn_Wv': _L0_gnn_in['Wv'], 'L0_gnn_bv': _L0_gnn_in['bv'], 'L0_gnn_Wo': _L0_gnn_in['Wo'], 'L0_gnn_bo': _L0_gnn_in['bo']}

def reference(x, adj, L0_gnn_Wq, L0_gnn_bq, L0_gnn_Wk, L0_gnn_bk, L0_gnn_Wv, L0_gnn_bv, L0_gnn_Wo, L0_gnn_bo):
    import jax
    import jax.numpy as jnp

    def _L0_gnn_ref(x, adj, Wq, bq, Wk, bk, Wv, bv, Wo, bo):
        import jax, jax.numpy as jnp
        import numpy as np
        B, N, D, H = (4, 1024, 256, 8)
        HD = D // H
        b, n, d = x.shape
        q = (x @ Wq + bq).reshape(b, n, H, HD)
        k = (x @ Wk + bk).reshape(b, n, H, HD)
        v = (x @ Wv + bv).reshape(b, n, H, HD)
        scores = jnp.einsum('bqhd,bkhd->bhqk', q, k) / jnp.sqrt(jnp.float32(HD))
        scores = scores + (1.0 - adj)[None, None, :, :] * -1000000000.0
        attn = jax.nn.softmax(scores, axis=-1)
        out = jnp.einsum('bhqk,bkhd->bqhd', attn, v).reshape(b, n, d)
        return out @ Wo + bo
    h = jnp.maximum(_layernorm(x, axis=-1), 0.0)
    x = x + _L0_gnn_ref(h, adj, L0_gnn_Wq, L0_gnn_bq, L0_gnn_Wk, L0_gnn_bk, L0_gnn_Wv, L0_gnn_bv, L0_gnn_Wo, L0_gnn_bo)
    return x

_drawn_inputs = setup_inputs


def setup_inputs(seed=0):
    import zlib

    import numpy as np

    out = dict(_drawn_inputs(seed))
    spreads = {'L0_gnn_bq': (0.0, 0.8),
     'L0_gnn_bk': (0.0, 0.8),
     'L0_gnn_bv': (0.0, 0.1),
     'L0_gnn_bo': (0.0, 0.1)}
    factors = {}
    for name, (base, spread) in spreads.items():
        noise = np.random.default_rng([zlib.crc32(name.encode()), seed]).standard_normal(out[name].shape)
        drawn = base * np.exp(spread * noise) if base else spread * noise
        out[name] = jnp.asarray(drawn.astype(out[name].dtype))
    for name, factor in factors.items():
        out[name] = (out[name] * factor).astype(out[name].dtype)
    return out
```

```python
from contextlib import ExitStack

import concourse.bass as bass
from concourse import mybir

ALU = mybir.AluOpType
ACT = mybir.ActivationFunctionType
F32 = mybir.dt.float32
F32R = mybir.dt.float32r

P = 128
HEADS = 8
GROUP = 4
EPS = 1e-5
BIG = 1e9
HUGE = 3.0e38

SCORES_AHEAD = 4
MASK_AHEAD = 3
EXP_AHEAD = 2
RING = 4

MIX_AT = 1
STATS_AT = (3, 4)
VARIANCE_AT = 5
RECIP_SUM_AT = (14, 30)
RECIP_AT = (18, 2)
ATTN_AT = (19, 3)
OUT_AT = (5, 7)
TURN_H_AT = (9, 11)
Q_AT = (12, 20)
K_AT = (14, 22)
V_AT = (24, 26)


def graph_attention(nc, x, adj, wq, bq, wk, bk, wv, bv, wo, bo, out):
    NB, N, D = x.shape
    HD = D // HEADS
    R = N // P
    C = D // P
    TILES = HEADS * R
    GRAINS = TILES // GROUP
    GT = GROUP * R
    SCALE = float(HD) ** -0.5
    assert HD == 32 and R == 4 and C == 2 and GROUP * HD == P and NB % 2 == 0

    x_rows = x.rearrange("b (p r) d -> b p r d", r=R)
    out_rows = out.rearrange("b (p r) d -> b p r d", r=R)

    with ExitStack() as ctx:
        def sb(name, shape, dt=F32):
            return ctx.enter_context(nc.sbuf_tensor(name, shape, dt))

        def psum(name, shape):
            return ctx.enter_context(nc.psum_tensor(name, shape, F32))

        def sem(name):
            return ctx.enter_context(nc.semaphore(name))

        ident = sb("ident", [P, P])
        minus_half = sb("minus_half", [P, R])
        mask = sb("mask", [P, R, N])
        w_q, w_k, w_v, w_o = (sb(n, [P, C, D]) for n in ("w_q", "w_k", "w_v", "w_o"))
        bias_q = sb("bias_q", [P, C])
        bias_qs = sb("bias_qs", [P, C])
        bias_k = sb("bias_k", [P, C])
        bias_v = sb("bias_v", [P, D])
        bias_o = sb("bias_o", [P, D])
        adj_in = sb("adj_in", [P, R, N])
        x_in = sb("x_in", [P, R, D])
        residual = sb("residual", [P, 2, R, D])
        bn = sb("bn", [P, R, 6])
        meanvar = sb("meanvar", [P, R, 2])
        variance = sb("variance", [P, R])
        rstd = sb("rstd", [P, R])
        h = sb("h", [P, R, D])
        hT = sb("hT", [P, C, N])
        full = sb("full", [P, 2, N])
        split = sb("split", [P, C, 4, N], F32R)
        stack = sb("stack", [P, 2, HEADS, 2, N], F32R)
        v = sb("v", [P, 2, R, D])
        masked = sb("masked", [P, RING, N])
        negmax = sb("negmax", [P, TILES])
        probs = sb("probs", [P, RING, N])
        sums = sb("sums", [P, 2, TILES])
        probsT = sb("probsT", [P, 2, GROUP, R, P])
        recip = sb("recip", [P, 2, GT])
        recip_wide = sb("recip_wide", [P, R, GROUP, HD])
        recipT = sb("recipT", [P, N])
        attnT = sb("attnT", [P, 2, N])
        y = sb("y", [P, R, D])

        ps_scores = psum("ps_scores", [P, RING, N])
        ps_turned = psum("ps_turned", [P, 2, R, P])
        ps_mixed = psum("ps_mixed", [P, R, P])
        ps_misc = psum("ps_misc", [P, N])

        const_loaded, bias_loaded = sem("const_loaded"), sem("bias_loaded")
        ident_made, bias_scaled, mask_made = sem("ident_made"), sem("bias_scaled"), sem("mask_made")
        x_loaded = sem("x_loaded")
        bn_made, meanvar_made = sem("bn_made"), sem("meanvar_made")
        variance_made, rstd_made = sem("variance_made"), sem("rstd_made")
        h_made, residual_made = sem("h_made"), sem("residual_made")
        hT_ready, hT_out_act, hT_out_dve = sem("hT_ready"), sem("hT_out_act"), sem("hT_out_dve")
        qk_ready, full_made, hi_made, split_made = sem("qk_ready"), sem("full_made"), sem("hi_made"), sem("split_made")
        stacked = [sem(f"stacked{g}") for g in range(2)]
        v_ready, v_made = sem("v_ready"), sem("v_made")
        scores_ready, masked_made, probs_made = sem("scores_ready"), sem("masked_made"), sem("probs_made")
        turned, turned_out_act, turned_out_dve = sem("turned"), sem("turned_out_act"), sem("turned_out_dve")
        mixed = sem("mixed")
        recip_made, recip_spread = sem("recip_made"), sem("recip_spread")
        recipT_ready, recipT_made = sem("recipT_ready"), sem("recipT_made")
        attnT_made, out_ready, y_made = sem("attnT_made"), sem("out_ready"), sem("y_made")
        y_stored = [sem(f"y_stored{i}") for i in range(2)]

        block = ctx.enter_context(nc.Block())

        def slots(eng, slot):
            slot(0, 0, True, False)
            with eng.Fori(0, NB // 2 - 1) as i:
                slot(i * 2 + 1, 1, False, False)
                slot(i * 2 + 2, 0, False, False)
            slot(NB - 1, 1, False, True)

        @block.sync
        def _(sp):
            def load_x(b):
                sp.dma_start(x_in[:], x_rows[b]).then_inc(x_loaded, 16)

            def stack_half(b, par, c):
                sp.wait_ge(split_made, b * 4 + 2 * c + 2)
                for j in range(GROUP):
                    for s, q_part, k_part in ((0, 0, 2), (1, 0, 3), (2, 1, 2), (3, 1, 3)):
                        src = split[HD * j:HD * j + HD, c, q_part:k_part + 1:k_part - q_part, :]
                        sp.dma_start(stack[HD * s:HD * s + HD, par, GROUP * c + j].bitcast(F32),
                                     src.bitcast(F32)).then_inc(stacked[c], 16)

            def store(b, half):
                sp.wait_ge(y_made, b * 2 + half + 1)
                sp.wait_ge(const_loaded, 64)
                sp.dma_start(out_rows[b][:, 2 * half:2 * half + 2, :],
                             y[:, 2 * half:2 * half + 2, :]).then_inc(y_stored[half], 16)

            def slot(b, par, first, last):
                if not last:
                    sp.wait_ge(residual_made, b + 1)
                    sp.wait_ge(const_loaded, 64)
                    load_x(b + 1)
                if not first:
                    store(b - 1, 0)
                    store(b - 1, 1)
                if not last:
                    if not first:
                        sp.wait_ge(scores_ready, b * TILES)
                        sp.wait_ge(const_loaded, 64)
                    stack_half(b + 1, 1 - par, 0)
                    stack_half(b + 1, 1 - par, 1)

            load_x(0)
            for dst, src in ((w_q, wq), (w_k, wk), (w_v, wv), (w_o, wo)):
                sp.dma_start(dst[:], src.rearrange("(c p) n -> p c n", p=P)).then_inc(const_loaded, 16)
            stack_half(0, 0, 0)
            stack_half(0, 0, 1)
            slots(sp, slot)
            store(NB - 1, 0)
            store(NB - 1, 1)
            sp.wait_ge(y_stored[0], 16 * NB)
            sp.wait_ge(y_stored[1], 16 * NB)

        @block.gpsimd
        def _(pool):
            def normalise(b):
                pool.wait_ge(meanvar_made, b * R + R)
                pool.nop(nofuse=True)
                pool.tensor_scalar(variance[:], meanvar[:, :, 1], EPS, None, ALU.add).then_inc(variance_made, 1)
                pool.wait_ge(variance_made, b + 1)
                pool.tensor_tensor(rstd[:], variance[:], minus_half[:], ALU.pow).then_inc(rstd_made, 1)
                pool.wait_ge(rstd_made, b + 1)
                if not isinstance(b, int) or b > 0:
                    pool.wait_ge(hT_ready, b * C)
                pool.nop(nofuse=True)
                for r in range(R):
                    pool.tensor_scalar(h[:, r], x_in[:, r], meanvar[:, r, 0:1], rstd[:, r:r + 1],
                                       ALU.subtract, ALU.mult).then_inc(h_made, 1)

            def add_residual(b, par, fresh):
                if not fresh:
                    pool.wait_ge(y_made, b * 2 - 2)
                pool.tensor_tensor(residual[:, par], x_in[:], bias_o[:].unsqueeze(1).to_broadcast([P, R, D]),
                                   ALU.add).then_inc(residual_made, 1)

            def split_parts(b, c, i):
                n = b * 4 + 2 * c + i + 1
                pool.wait_ge(full_made, n)
                if not isinstance(b, int) or b > 0:
                    pool.wait_ge(stacked[c], b * (256))
                hi, lo = split[:, c, 2 * i], split[:, c, 2 * i + 1]
                pool.nop(nofuse=True)
                pool.tensor_copy(hi, full[:, i]).then_inc(hi_made, 1)
                pool.wait_ge(hi_made, n)
                pool.tensor_tensor(lo, full[:, i], hi.bitcast(F32), ALU.subtract).then_inc(split_made, 1)

            def spread_recip(b, g, fresh):
                pool.wait_ge(recip_made, b * 2 + g + 1)
                if not fresh:
                    pool.wait_ge(recipT_ready, b * 2 + g)
                pool.nop(nofuse=True)
                pool.tensor_copy(recip_wide[:], recip[:, g].rearrange("p (r j) -> p r j", j=GROUP)
                                 .unsqueeze(3).to_broadcast([P, R, GROUP, HD])).then_inc(recip_spread, 1)

            def slot(b, par, first, last):
                if not first:
                    spread_recip(b - 1, 1, False)
                if not last:
                    normalise(b + 1)
                    add_residual(b + 1, 1 - par, first)
                    split_parts(b + 1, 0, 0)
                    split_parts(b + 1, 0, 1)
                spread_recip(b, 0, first)
                if not last:
                    split_parts(b + 1, 1, 0)
                    split_parts(b + 1, 1, 1)

            pool.memset(ident[:], 0.0).then_inc(ident_made, 1)
            pool.memset(minus_half[:], -0.5).then_inc(ident_made, 1)
            pool.wait_ge(ident_made, 2)
            pool.affine_select(out=ident[:], in_=ident[:], compare_op=ALU.not_equal, fill=1.0, base=0,
                               pattern=[[-1, P]], channel_multiplier=1).then_inc(ident_made, 1)
            pool.wait_ge(bias_loaded, 80)
            pool.tensor_scalar(bias_qs[:], bias_q[:], SCALE, None, ALU.mult).then_inc(bias_scaled, 1)
            normalise(0)
            for r in range(R):
                pool.tensor_scalar(mask[:, r].rearrange("p (k q) -> p k q", k=R),
                                   adj_in[:, r].rearrange("p (q k) -> p k q", k=R),
                                   1.0, BIG, ALU.subtract, ALU.mult).then_inc(mask_made, 1)
            add_residual(0, 0, True)
            for c in range(C):
                split_parts(0, c, 0)
                split_parts(0, c, 1)
            slots(pool, slot)
            spread_recip(NB - 1, 1, False)

        @block.scalar
        def _(act):
            def exponentials(b, par, u):
                t = b * TILES + u
                w = u % TILES
                act.wait_ge(masked_made, t + 1)
                if not isinstance(b, int) or t >= RING:
                    act.wait_ge(turned, t + 1 - RING)
                act.activation(probs[:, w % RING], masked[:, w % RING], ACT.Exp, scale=-1.0,
                               bias=negmax[:, w:w + 1],
                               accum_out=sums[:, par, w:w + 1]).then_inc(probs_made, 1)

            def take_turned(b, u, first):
                grain, j = u // GROUP, u % GROUP
                act.wait_ge(turned, b * TILES + u + 1)
                if not first or grain >= 2:
                    act.wait_ge(mixed, b * GRAINS + grain - 1)
                act.copy(probsT[:, grain % 2, j], ps_turned[:, u % 2]).then_inc(turned_out_act, 1)

            def take_hT(b):
                act.wait_ge(hT_ready, b * C + 1)
                act.activation(hT[:, 0], ps_misc[:], ACT.Relu).then_inc(hT_out_act, 1)

            def take_qk(b, c, i, fresh):
                act.wait_ge(qk_ready, b * 4 + 2 * c + i + 1)
                if not fresh:
                    act.wait_ge(split_made, b * 4 + 2 * c + i - 1)
                if i == 0:
                    act.activation(full[:, 0], ps_misc[:], ACT.Identity, scale=SCALE,
                                   bias=bias_qs[:, c:c + 1]).then_inc(full_made, 1)
                else:
                    act.activation(full[:, 1], ps_misc[:], ACT.Identity,
                                   bias=bias_k[:, c:c + 1]).then_inc(full_made, 1)

            def take_recipT(b, g, fresh):
                act.wait_ge(recipT_ready, b * 2 + g + 1)
                if not fresh:
                    act.wait_ge(attnT_made, b * 2 + g)
                act.copy(recipT[:], ps_misc[:]).then_inc(recipT_made, 1)

            def slot(b, par, first, last):
                for u in range(TILES):
                    ahead = u + EXP_AHEAD
                    if not last or ahead < TILES:
                        exponentials(b, par ^ (ahead >= TILES), ahead)
                    if u % 2 == 0:
                        take_turned(b, u, first)
                    if u == RECIP_AT[1] and not first:
                        take_recipT(b - 1, 1, False)
                    if u == RECIP_AT[0]:
                        take_recipT(b, 0, first)
                    if not last:
                        if u == TURN_H_AT[0]:
                            take_hT(b + 1)
                        for c in range(C):
                            if u == Q_AT[c] + 1:
                                take_qk(b + 1, c, 0, False)
                            if u == K_AT[c] + 1:
                                take_qk(b + 1, c, 1, False)

            act.dma_start(bias_q[:], bq.rearrange("(c p) -> p c", p=P), allow_slow_non_contiguous=True).then_inc(bias_loaded, 16)
            act.dma_start(bias_k[:], bk.rearrange("(c p) -> p c", p=P), allow_slow_non_contiguous=True).then_inc(bias_loaded, 16)
            act.dma_start(bias_v[:], bv.unsqueeze(0).to_broadcast([P, D])).then_inc(bias_loaded, 16)
            act.dma_start(bias_o[:], bo.unsqueeze(0).to_broadcast([P, D])).then_inc(bias_loaded, 16)
            act.dma_start(adj_in[:], adj.rearrange("(p r) k -> p r k", r=R)).then_inc(bias_loaded, 16)
            take_hT(0)
            act.wait_ge(bias_scaled, 1)
            act.wait_ge(bias_loaded, 80)
            for c in range(C):
                take_qk(0, c, 0, c == 0)
                take_qk(0, c, 1, c == 0)
            for u in range(EXP_AHEAD):
                exponentials(0, 0, u)
            slots(act, slot)
            take_recipT(NB - 1, 1, False)

        @block.vector
        def _(dve):
            def statistics(b, rows):
                if rows[0] == 0:
                    dve.wait_ge(x_loaded, b * 16 + 16)
                for r in rows:
                    dve.bn_stats(bn[:, r], x_in[:, r]).then_inc(bn_made, 1)

            def mean_and_variance(b):
                dve.wait_ge(bn_made, b * R + R)
                if not isinstance(b, int) or b > 0:
                    dve.wait_ge(h_made, b * R)
                dve.nop(nofuse=True)
                for r in range(R):
                    dve.bn_aggr(meanvar[:, r], bn[:, r]).then_inc(meanvar_made, 1)

            def mask_tile(b, u):
                t = b * TILES + u
                w = u % TILES
                r = w // GROUP % R
                dve.wait_ge(scores_ready, t + 1)
                if not isinstance(b, int) or t >= RING:
                    dve.wait_ge(probs_made, t + 1 - RING)
                dve.nop(nofuse=True)
                dve.tensor_tensor_reduce(out=masked[:, w % RING], in0=ps_scores[:, w % RING],
                                         in1=mask[:, r], scale=-1.0, scalar=HUGE, op0=ALU.add,
                                         op1=ALU.min, accum_out=negmax[:, w:w + 1]).then_inc(masked_made, 1)

            def take_turned(b, u, first):
                grain, j = u // GROUP, u % GROUP
                dve.wait_ge(turned, b * TILES + u + 1)
                if not first or grain >= 2:
                    dve.wait_ge(mixed, b * GRAINS + grain - 1)
                dve.tensor_copy(probsT[:, grain % 2, j], ps_turned[:, u % 2]).then_inc(turned_out_dve, 1)

            def take_hT(b):
                dve.wait_ge(hT_ready, b * C + 2)
                dve.tensor_scalar(hT[:, 1], ps_misc[:], 0.0, None, ALU.max).then_inc(hT_out_dve, 1)

            def take_v(b, par, half):
                dve.wait_ge(v_ready, b * 2 + half + 1)
                dve.tensor_tensor(v[:, par, 2 * half:2 * half + 2], ps_misc[:].rearrange("p (r d) -> p r d", r=2),
                                  bias_v[:].unsqueeze(1).to_broadcast([P, 2, D]), ALU.add).then_inc(v_made, 1)

            def invert_sums(b, par, g, first):
                dve.wait_ge(probs_made, b * TILES + GT * (g + 1))
                if not first:
                    dve.wait_ge(recip_spread, b * 2 + g - 1)
                dve.reciprocal(recip[:, g], sums[:, par, GT * g:GT * g + GT]).then_inc(recip_made, 1)

            def divide(b, g):
                dve.wait_ge(mixed, b * GRAINS + R * (g + 1))
                dve.wait_ge(recipT_made, b * 2 + g + 1)
                dve.tensor_tensor(attnT[:, g], ps_mixed[:].rearrange("p r q -> p (r q)"), recipT[:],
                                  ALU.mult).then_inc(attnT_made, 1)

            def take_y(b, par, half, fresh):
                dve.wait_ge(out_ready, b * 2 + half + 1)
                dve.wait_ge(residual_made, b + 1)
                if not fresh:
                    dve.wait_ge(y_stored[half], b * 16)
                dve.tensor_tensor(y[:, 2 * half:2 * half + 2], ps_misc[:].rearrange("p (r d) -> p r d", r=2),
                                  residual[:, par, 2 * half:2 * half + 2], ALU.add).then_inc(y_made, 1)

            def slot(b, par, first, last):
                for u in range(TILES):
                    ahead = u + MASK_AHEAD
                    if not last or ahead < TILES:
                        mask_tile(b, ahead)
                    if u % 2 == 1:
                        take_turned(b, u, first)
                    for g in range(2):
                        if u == RECIP_SUM_AT[g]:
                            invert_sums(b, par, g, first)
                    if u == ATTN_AT[1] and not first:
                        divide(b - 1, 1)
                    if u == ATTN_AT[0]:
                        divide(b, 0)
                    for half in range(2):
                        if u == OUT_AT[half] and not first:
                            take_y(b - 1, 1 - par, half, isinstance(b, int) and b == 1)
                    if not last:
                        for half in range(2):
                            if u == STATS_AT[half]:
                                statistics(b + 1, (2 * half, 2 * half + 1))
                            if u == V_AT[half]:
                                take_v(b + 1, 1 - par, half)
                        if u == VARIANCE_AT:
                            mean_and_variance(b + 1)
                        if u == TURN_H_AT[1]:
                            take_hT(b + 1)

            statistics(0, range(R))
            mean_and_variance(0)
            take_hT(0)
            dve.wait_ge(bias_loaded, 80)
            take_v(0, 0, 0)
            take_v(0, 0, 1)
            dve.wait_ge(mask_made, R)
            for u in range(MASK_AHEAD):
                mask_tile(0, u)
            slots(dve, slot)
            divide(NB - 1, 1)
            take_y(NB - 1, 1, 0, False)
            take_y(NB - 1, 1, 1, False)

        @block.tensor
        def _(pe):
            def scores(b, par, u):
                t = b * TILES + u
                w = u % TILES
                g, r, j = w // GT, w // GROUP % R, w % GROUP
                if r == 0 and j == 0:
                    pe.wait_ge(stacked[g], (b + u // TILES) * 256 + 256)
                if not isinstance(b, int) or t >= RING:
                    pe.wait_ge(masked_made, t + 1 - RING)
                pe.matmul(ps_scores[:, w % RING], stack[:, par, GROUP * g + j, 0, r * P:r * P + P],
                          stack[:, par, GROUP * g + j, 1], start=True, stop=True).then_inc(scores_ready, 1)

            def turn(b, u, first):
                t = b * TILES + u
                pe.wait_ge(probs_made, t + 1)
                if not first or u >= 2:
                    before = b * (TILES // 2) + u // 2
                    pe.wait_ge(turned_out_act if u % 2 == 0 else turned_out_dve, before)
                for k in range(R):
                    last = pe.transpose(ps_turned[:, u % 2, k], probs[:, u % RING, k * P:k * P + P], ident[:])
                last.then_inc(turned, 1)

            def mix(b, par, grain, first):
                g, r = grain // R, grain % R
                pe.wait_ge(turned_out_act, b * (TILES // 2) + 2 * grain + 2)
                pe.wait_ge(turned_out_dve, b * (TILES // 2) + 2 * grain + 2)
                pe.wait_ge(v_made, b * 2 + 2)
                if r == 0 and not (first and g == 0):
                    pe.wait_ge(attnT_made, b * 2 + g)
                for k in range(R):
                    for j in range(GROUP):
                        head = GROUP * g + j
                        last = pe.matmul(ps_mixed[HD * j:HD * j + HD, r], v[:, par, k, head * HD:head * HD + HD],
                                         probsT[:, grain % 2, j, k], start=(k == 0), stop=(k == R - 1))
                last.then_inc(mixed, 1)

            def turn_recip(b, g):
                pe.wait_ge(recip_spread, b * 2 + g + 1)
                for r in range(R):
                    last = pe.transpose(ps_misc[:, r * P:r * P + P],
                                        recip_wide[:, r].rearrange("p j d -> p (j d)"), ident[:])
                last.then_inc(recipT_ready, 1)

            def project_out(b, half):
                pe.wait_ge(attnT_made, b * 2 + 2)
                for i in range(2):
                    r = 2 * half + i
                    for g in range(2):
                        last = pe.matmul(ps_misc[:, i * D:i * D + D], attnT[:, g, r * P:r * P + P], w_o[:, g],
                                         start=(g == 0), stop=(g == 1))
                last.then_inc(out_ready, 1)

            def turn_h(b, c):
                pe.wait_ge(h_made, b * R + R)
                for r in range(R):
                    last = pe.transpose(ps_misc[:, r * P:r * P + P], h[:, r, c * P:c * P + P], ident[:])
                last.then_inc(hT_ready, 1)

            def project_qk(b, w, half, c):
                m = pe.matmul(ps_misc[:], w[:, c, half * P:half * P + P], hT[:, c],
                              start=(c == 0), stop=(c == C - 1))
                if c == C - 1:
                    m.then_inc(qk_ready, 1)

            def project_v(b, half):
                for i in range(2):
                    r = 2 * half + i
                    for c in range(C):
                        last = pe.matmul(ps_misc[:, i * D:i * D + D], hT[:, c, r * P:r * P + P], w_v[:, c],
                                         start=(c == 0), stop=(c == C - 1))
                last.then_inc(v_ready, 1)

            def piece_of_last(b, u):
                if u == RECIP_AT[1]:
                    turn_recip(b, 1)
                if u == OUT_AT[0]:
                    pe.wait_ge(recipT_made, b * 2 + 2)
                    project_out(b, 0)
                if u == OUT_AT[1]:
                    pe.wait_ge(y_made, b * 2 + 1)
                    project_out(b, 1)

            def piece_of_next(b, u, first):
                if u == TURN_H_AT[0]:
                    if not first:
                        pe.wait_ge(y_made, b * 2 - 2)
                    turn_h(b, 0)
                if u == TURN_H_AT[1]:
                    pe.wait_ge(hT_out_act, b + 1)
                    turn_h(b, 1)
                if u == Q_AT[0]:
                    pe.wait_ge(hT_out_act, b + 1)
                    pe.wait_ge(hT_out_dve, b + 1)
                if u == K_AT[0]:
                    pe.wait_ge(full_made, b * 4 + 1)
                if u == K_AT[1]:
                    pe.wait_ge(full_made, b * 4 + 3)
                for half in range(2):
                    for c in range(C):
                        if u == Q_AT[half] + c:
                            project_qk(b, w_q, half, c)
                        if u == K_AT[half] + c:
                            project_qk(b, w_k, half, c)
                if u == V_AT[0]:
                    pe.wait_ge(full_made, b * 4 + 4)
                    project_v(b, 0)
                if u == V_AT[1]:
                    pe.wait_ge(v_made, b * 2 + 1)
                    project_v(b, 1)

            def slot(b, par, first, last):
                for u in range(TILES):
                    ahead = u + SCORES_AHEAD
                    if not last or ahead < TILES:
                        scores(b, par ^ (ahead >= TILES), ahead)
                    turn(b, u, first)
                    if u % GROUP == MIX_AT:
                        if u >= GROUP:
                            mix(b, par, u // GROUP - 1, first)
                        elif not first:
                            mix(b - 1, 1 - par, GRAINS - 1, False)
                    if not first:
                        if u == RECIP_AT[1]:
                            pe.wait_ge(v_made, b * 2 + 2)
                        piece_of_last(b - 1, u)
                    if u == RECIP_AT[0]:
                        if last:
                            pe.wait_ge(y_made, b * 2)
                        else:
                            pe.wait_ge(full_made, b * 4 + 4 + 2)
                        turn_recip(b, 0)
                    if not last:
                        if u == Q_AT[1]:
                            pe.wait_ge(recipT_made, b * 2 + 1)
                        if u == TURN_H_AT[0] and first:
                            pe.wait_ge(v_made, 2)
                        piece_of_next(b + 1, u, first)

            pe.wait_ge(ident_made, 3)
            pe.wait_ge(const_loaded, 64)
            for u in range(TILES):
                if u == Q_AT[1]:
                    pe.wait_ge(full_made, 2)
                piece_of_next(0, u, True)
            for u in range(SCORES_AHEAD):
                scores(0, 0, u)
            slots(pe, slot)
            mix(NB - 1, 1, GRAINS - 1, False)
            pe.wait_ge(recipT_made, NB * 2 - 1)
            for u in (RECIP_AT[1], *OUT_AT):
                piece_of_last(NB - 1, u)


_INS = ["x", "adj", "L0_gnn_Wq", "L0_gnn_bq", "L0_gnn_Wk", "L0_gnn_bk", "L0_gnn_Wv", "L0_gnn_bv",
        "L0_gnn_Wo", "L0_gnn_bo"]


def kernel(**inputs):
    import concourse.bacc as bacc
    import numpy as np
    from concourse.bass_utils import run_bass_kernel_spmd

    nc = bacc.Bacc("TRN2", target_bir_lowering=False, num_devices=1)
    arrays, args = {}, []
    for name in _INS:
        a = np.ascontiguousarray(inputs[name])
        arrays[f"in_{name}_dram"] = a
        args.append(nc.dram_tensor(f"in_{name}_dram", a.shape, mybir.dt.from_np(a.dtype), kind="ExternalInput").ap())
    shape = inputs["x"].shape
    args.append(nc.dram_tensor("out_0_dram", shape, F32, kind="ExternalOutput").ap())
    graph_attention(nc, *args)
    r = run_bass_kernel_spmd(nc, [arrays], core_ids=[0])
    return r.results[0]["out_0_dram"]
```

```python
from contextlib import ExitStack

import concourse.bass as bass
from concourse import mybir

ALU = mybir.AluOpType
ACT = mybir.ActivationFunctionType
F32 = mybir.dt.float32
F32R = mybir.dt.float32r

P = 128
HEADS = 8
GROUP = 4
EPS = 1e-5
STACKED = 16 * 16
BIG = 1e9
HUGE = 3.0e38

SCORES_AHEAD = 3
MASK_AHEAD = 3
EXP_AHEAD = 2
SCORE_BANKS = 3
RING = 4
DVE_TURNED = 3
MISC = 2

MIX_AT = (1, 2, 3, 4)
RECIP_1, TURN_H, Q_0, K_0, OUT_0, OUT_1, RECIP_0, Q_1, K_1, V_0, V_1 = 0, (1, 2), 3, 4, 5, 6, 7, 8, 9, 10, 11
RECIP_AT = (20, 2)
TURN_H_AT = (4, 5)
Q_AT = ((8, 9, 10), (21, 22, 23))
K_AT = ((11, 12, 13), (24, 25, 26))
OUT_AT = ((14, 15, 16), (17, 18, 19))
V_AT = ((27, 28, 28), (29, 30, 30))
STATS_AT = (0, 0)
VARIANCE_AT = 0
NORMAL_AT = 3
INVERT_AT = (15, 31)
DIVIDE_AT = (22, 5)
ATTN_HI_AT = (24, 7)


def graph_attention(nc, x, adj, wq, bq, wk, bk, wv, bv, wo, bo, out):
    NB, N, D = x.shape
    HD = D // HEADS
    R = N // P
    C = D // P
    TILES = HEADS * R
    GRAINS = TILES // GROUP
    GT = GROUP * R
    SCALE = float(HD) ** -0.5
    assert HD == 32 and R == 4 and C == 2 and GROUP * HD == P and NB % 2 == 0

    x_rows = x.rearrange("b (p r) d -> b p r d", r=R)
    out_rows = out.rearrange("b (p r) d -> b p r d", r=R)

    with ExitStack() as ctx:
        def sb(name, shape, dt=F32):
            return ctx.enter_context(nc.sbuf_tensor(name, shape, dt))

        def psum(name, shape):
            return ctx.enter_context(nc.psum_tensor(name, shape, F32))

        def sem(name):
            return ctx.enter_context(nc.semaphore(name))

        ident = sb("ident", [P, P])
        minus_half = sb("minus_half", [P, R])
        mask = sb("mask", [P, R, N])
        w_q, w_k, w_v, w_o = (sb(n, [P, 2, C, D], F32R) for n in ("w_q", "w_k", "w_v", "w_o"))
        bias_q = sb("bias_q", [P, C])
        bias_qs = sb("bias_qs", [P, C])
        bias_k = sb("bias_k", [P, C])
        bias_v = sb("bias_v", [P, D])
        bias_o = sb("bias_o", [P, D])
        x_in = sb("x_in", [P, R, D])
        residual = sb("residual", [P, 2, R, D])
        bn = sb("bn", [P, R, 6])
        meanvar = sb("meanvar", [P, R, 2])
        variance = sb("variance", [P, R])
        rstd = sb("rstd", [P, R])
        h = sb("h", [P, R, D])
        hT = sb("hT", [P, 2, C, N], F32R)
        full = sb("full", [P, 2, N])
        split = sb("split", [P, C, 4, N], F32R)
        stack = sb("stack", [P, 2, HEADS, 2, N], F32R)
        v = sb("v", [P, 2, R, D])
        masked = sb("masked", [P, RING, N])
        negmax = sb("negmax", [P, TILES])
        probs = sb("probs", [P, RING, N])
        sums = sb("sums", [P, 2, TILES])
        probsT = sb("probsT", [P, 4, GROUP, R, P])
        adj_in = probsT[:, 3].rearrange("p j k q -> p (j k q)").rearrange("p (r n) -> p r n", r=R)
        w_in = probsT[:, 2, 0:2].rearrange("p j k q -> p (j k q)").rearrange("p (i c d) -> p i c d", i=2, c=C)
        recip = sb("recip", [P, GT])
        recip_wide = sb("recip_wide", [P, R, GROUP, HD])
        recipT = sb("recipT", [P, N])
        attn_full = sb("attn_full", [P, 2, N])
        attnT = sb("attnT", [P, 2, 2, N], F32R)

        ps_scores = psum("ps_scores", [P, SCORE_BANKS, N])
        ps_turned = psum("ps_turned", [P, 2, R, P])
        ps_mixed = psum("ps_mixed", [P, R, P])
        ps_misc = psum("ps_misc", [P, MISC, N])

        w_loaded = [sem(f"w_loaded{i}") for i in range(4)]
        bias_loaded = sem("bias_loaded")
        ident_made, bias_scaled, mask_made = sem("ident_made"), sem("bias_scaled"), sem("mask_made")
        x_loaded = sem("x_loaded")
        bn_made, meanvar_made = sem("bn_made"), sem("meanvar_made")
        variance_made, rstd_made = sem("variance_made"), sem("rstd_made")
        h_made, residual_made = sem("h_made"), sem("residual_made")
        hT_ready, hT_hi_made, hT_lo_made = sem("hT_ready"), sem("hT_hi_made"), sem("hT_lo_made")
        qk_ready, full_made, hi_made, split_made = sem("qk_ready"), sem("full_made"), sem("hi_made"), sem("split_made")
        stacked = [sem(f"stacked{g}") for g in range(2)]
        v_ready, v_made = sem("v_ready"), sem("v_made")
        scores_ready, masked_made, probs_made = sem("scores_ready"), sem("masked_made"), sem("probs_made")
        turned, turned_out_act, turned_out_dve = sem("turned"), sem("turned_out_act"), sem("turned_out_dve")
        mixed = sem("mixed")
        recip_made, recip_spread, w_hi_made, w_split = sem("recip_made"), sem("recip_spread"), sem("w_hi_made"), sem("w_split")
        recipT_ready, recipT_made = sem("recipT_ready"), sem("recipT_made")
        divided, attn_hi_made, attn_lo_made = sem("divided"), sem("attn_hi_made"), sem("attn_lo_made")
        out_ready, y_made = sem("out_ready"), sem("y_made")
        y_stored = [sem(f"y_stored{i}") for i in range(2)]

        def bank(place):
            return ps_misc[:, place % MISC]

        def last_in_bank(w):
            return (TILES - 1 - w % SCORE_BANKS) // SCORE_BANKS * SCORE_BANKS + w % SCORE_BANKS

        def row_tiles(ap):
            return ap.rearrange("p (r d) -> p r d", r=2)

        block = ctx.enter_context(nc.Block())

        def slots(eng, slot):
            slot(0, 0, True, False)
            with eng.Fori(0, NB // 2 - 1) as i:
                slot(i * 2 + 1, 1, False, False)
                slot(i * 2 + 2, 0, False, False)
            slot(NB - 1, 1, False, True)

        @block.sync
        def _(sp):
            def load_x(b):
                sp.dma_start(x_in[:], x_rows[b]).then_inc(x_loaded, 16)

            def load_x_when_free(b):
                sp.wait_ge(residual_made, b)
                sp.nop(nofuse=True)
                sp.wait_ge(h_made, b)
                sp.nop(nofuse=True)
                load_x(b)

            def stack_half(b, par, c):
                sp.wait_ge(split_made, b * 4 + 2 * c + 2)
                sp.nop(nofuse=True)
                for j in range(GROUP):
                    for s, q_part, k_part in ((0, 0, 2), (1, 0, 3), (2, 1, 2), (3, 1, 3)):
                        src = split[HD * j:HD * j + HD, c, q_part:k_part + 1:k_part - q_part, :]
                        sp.dma_start(stack[HD * s:HD * s + HD, par, GROUP * c + j].bitcast(F32),
                                     src.bitcast(F32)).then_inc(stacked[c], 16)

            def store(b, par, half):
                sp.wait_ge(y_made, b * 2 + half + 1)
                sp.nop(nofuse=True)
                sp.dma_start(out_rows[b][:, 2 * half:2 * half + 2, :],
                             residual[:, par, 2 * half:2 * half + 2, :]).then_inc(y_stored[half], 16)

            def slot(b, par, first, last, load=True):
                if not last:
                    if not first:
                        sp.wait_ge(scores_ready, b * TILES)
                        sp.nop(nofuse=True)
                    stack_half(b + 1, 1 - par, 0)
                if not first:
                    store(b - 1, 1 - par, 0)
                    store(b - 1, 1 - par, 1)
                if not last:
                    if load:
                        load_x_when_free(b + 2)
                    stack_half(b + 1, 1 - par, 1)

            load_x(0)
            sp.dma_start(w_in[:, 0], wq.rearrange("(c p) n -> p c n", p=P)).then_inc(w_loaded[0], 16)
            sp.dma_start(w_in[:, 1], wk.rearrange("(c p) n -> p c n", p=P)).then_inc(w_loaded[1], 16)
            for i, src in enumerate((wv, wo)):
                sp.wait_ge(w_split, i + 1)
                sp.dma_start(w_in[:, i], src.rearrange("(c p) n -> p c n", p=P)).then_inc(w_loaded[2 + i], 16)
            load_x_when_free(1)
            stack_half(0, 0, 0)
            stack_half(0, 0, 1)
            slot(0, 0, True, False)
            with sp.Fori(0, NB // 2 - 2) as i:
                slot(i * 2 + 1, 1, False, False)
                slot(i * 2 + 2, 0, False, False)
            slot(NB - 3, 1, False, False)
            slot(NB - 2, 0, False, False, load=False)
            slot(NB - 1, 1, False, True)
            store(NB - 1, 1, 0)
            store(NB - 1, 1, 1)
            sp.wait_ge(y_stored[0], 16 * NB)
            sp.wait_ge(y_stored[1], 16 * NB)

        @block.gpsimd
        def _(pool):
            def inverse_deviation(b):
                pool.wait_ge(meanvar_made, b * R + R)
                if not isinstance(b, int) or b > 0:
                    pool.wait_ge(h_made, b)
                pool.nop(nofuse=True)
                pool.tensor_scalar(variance[:], meanvar[:, :, 1], EPS, None, ALU.add).then_inc(variance_made, 1)
                pool.wait_ge(variance_made, b + 1)
                pool.tensor_tensor(rstd[:], variance[:], minus_half[:], ALU.pow).then_inc(rstd_made, 1)

            def add_residual(b, par, fresh):
                pool.wait_ge(x_loaded, b * 16 + 16)
                if not fresh:
                    pool.wait_ge(y_stored[0], b * 16 - 16)
                    pool.wait_ge(y_stored[1], b * 16 - 16)
                pool.tensor_tensor(residual[:, par], x_in[:], bias_o[:].unsqueeze(1).to_broadcast([P, R, D]),
                                   ALU.add).then_inc(residual_made, 1)

            def lo_part(b, c, i):
                pool.wait_ge(hi_made, b * 4 + 2 * c + i + 1)
                pool.tensor_tensor(split[:, c, 2 * i + 1], full[:, i], split[:, c, 2 * i].bitcast(F32),
                                   ALU.subtract).then_inc(split_made, 1)

            def attn_lo(b, g):
                pool.wait_ge(attn_hi_made, b * 2 + g + 1)
                if not isinstance(b, int) or b > 0:
                    pool.wait_ge(out_ready, b * 2)
                pool.tensor_tensor(attnT[:, 1, g], attn_full[:, g], attnT[:, 0, g].bitcast(F32),
                                   ALU.subtract).then_inc(attn_lo_made, 1)

            def slot(b, par, first, last):
                if not last:
                    inverse_deviation(b + 1)
                if not first:
                    attn_lo(b - 1, 1)
                if not last:
                    lo_part(b + 1, 0, 0)
                    lo_part(b + 1, 0, 1)
                    add_residual(b + 1, 1 - par, first)
                attn_lo(b, 0)
                if not last:
                    lo_part(b + 1, 1, 0)
                    lo_part(b + 1, 1, 1)

            pool.memset(ident[:], 0.0).then_inc(ident_made, 1)
            pool.memset(minus_half[:], -0.5).then_inc(ident_made, 1)
            pool.wait_ge(ident_made, 2)
            pool.affine_select(out=ident[:], in_=ident[:], compare_op=ALU.not_equal, fill=1.0, base=0,
                               pattern=[[-1, P]], channel_multiplier=1).then_inc(ident_made, 1)
            inverse_deviation(0)
            pool.wait_ge(bias_loaded, 80)
            pool.tensor_scalar(bias_qs[:], bias_q[:], SCALE, None, ALU.mult).then_inc(bias_scaled, 1)
            add_residual(0, 0, True)
            for c in range(C):
                lo_part(0, c, 0)
                lo_part(0, c, 1)
            slots(pool, slot)
            attn_lo(NB - 1, 1)

        @block.scalar
        def _(act):
            def exponentials(b, par, u):
                t = b * TILES + u
                w = u % TILES
                act.wait_ge(masked_made, t + 1)
                if not isinstance(b, int) or t >= RING:
                    act.wait_ge(turned, t + 1 - RING)
                act.activation(probs[:, w % RING], masked[:, w % RING], ACT.Exp, scale=-1.0,
                               bias=negmax[:, w:w + 1],
                               accum_out=sums[:, par, w:w + 1]).then_inc(probs_made, 1)

            def take_turned(b, u, first):
                grain, j = u // GROUP, u % GROUP
                act.wait_ge(turned, b * TILES + u + 1)
                if not first or grain >= 4:
                    act.wait_ge(mixed, b * (GRAINS // 2) + grain // 2 - 1)
                act.copy(probsT[:, grain % 4, j], ps_turned[:, u % 2]).then_inc(turned_out_act, 1)

            def hT_hi(b, c):
                act.wait_ge(hT_ready, b * C + c + 1)
                act.activation(hT[:, 0, c], bank(TURN_H[c]), ACT.Relu).then_inc(hT_hi_made, 1)

            def take_qk(b, c, i, fresh):
                act.wait_ge(qk_ready, b * 4 + 2 * c + i + 1)
                if not fresh:
                    act.wait_ge(split_made, b * 4 + 2 * c + i - 1)
                if i == 0:
                    act.activation(full[:, 0], bank((Q_0, Q_1)[c]), ACT.Identity, scale=SCALE,
                                   bias=bias_qs[:, c:c + 1]).then_inc(full_made, 1)
                else:
                    act.activation(full[:, 1], bank((K_0, K_1)[c]), ACT.Identity,
                                   bias=bias_k[:, c:c + 1]).then_inc(full_made, 1)

            def take_recipT(b, g, fresh):
                act.wait_ge(recipT_ready, b * 2 + g + 1)
                if not fresh:
                    act.wait_ge(divided, b * 2 + g)
                act.copy(recipT[:], bank((RECIP_0, RECIP_1)[g])).then_inc(recipT_made, 1)

            def attn_hi(b, g):
                act.wait_ge(divided, b * 2 + g + 1)
                if not isinstance(b, int) or b > 0:
                    act.wait_ge(out_ready, b * 2)
                act.copy(attnT[:, 0, g], attn_full[:, g]).then_inc(attn_hi_made, 1)

            def slot(b, par, first, last):
                for u in range(TILES):
                    ahead = u + EXP_AHEAD
                    if not last or ahead < TILES:
                        exponentials(b, par ^ (ahead >= TILES), ahead)
                    if u % GROUP != DVE_TURNED:
                        take_turned(b, u, first)
                    if not first:
                        if u == RECIP_AT[1] + 1:
                            take_recipT(b - 1, 1, False)
                        if u == ATTN_HI_AT[1]:
                            attn_hi(b - 1, 1)
                    if u == RECIP_AT[0] + 1:
                        take_recipT(b, 0, first)
                    if u == ATTN_HI_AT[0]:
                        attn_hi(b, 0)
                    if not last:
                        for c in range(C):
                            if u == TURN_H_AT[c] + 1:
                                hT_hi(b + 1, c)
                            if u == Q_AT[c][-1] + 1:
                                take_qk(b + 1, c, 0, False)
                            if u == K_AT[c][-1] + 1:
                                take_qk(b + 1, c, 1, False)

            act.dma_start(bias_q[:], bq.rearrange("(c p) -> p c", p=P),
                          allow_slow_non_contiguous=True).then_inc(bias_loaded, 16)
            act.dma_start(bias_k[:], bk.rearrange("(c p) -> p c", p=P),
                          allow_slow_non_contiguous=True).then_inc(bias_loaded, 16)
            act.dma_start(bias_v[:], bv.unsqueeze(0).to_broadcast([P, D])).then_inc(bias_loaded, 16)
            act.dma_start(bias_o[:], bo.unsqueeze(0).to_broadcast([P, D])).then_inc(bias_loaded, 16)
            act.dma_start(adj_in[:], adj.rearrange("(p r) k -> p r k", r=R)).then_inc(bias_loaded, 16)
            hT_hi(0, 0)
            hT_hi(0, 1)
            act.wait_ge(bias_scaled, 1)
            act.wait_ge(bias_loaded, 80)
            for c in range(C):
                take_qk(0, c, 0, c == 0)
                take_qk(0, c, 1, c == 0)
            for u in range(EXP_AHEAD):
                exponentials(0, 0, u)
            slots(act, slot)
            take_recipT(NB - 1, 1, False)
            attn_hi(NB - 1, 1)

        @block.vector
        def _(dve):
            def statistics(b, rows):
                if rows[0] == 0:
                    dve.wait_ge(x_loaded, b * 16 + 16)
                for r in rows:
                    dve.bn_stats(bn[:, r], x_in[:, r]).then_inc(bn_made, 1)

            def mean_and_variance(b):
                dve.wait_ge(bn_made, b * R + R)
                if not isinstance(b, int) or b > 0:
                    dve.wait_ge(variance_made, b)
                dve.nop(nofuse=True)
                for r in range(R):
                    dve.bn_aggr(meanvar[:, r], bn[:, r]).then_inc(meanvar_made, 1)

            def normalise(b):
                dve.wait_ge(meanvar_made, b * R + R)
                dve.wait_ge(rstd_made, b + 1)
                if not isinstance(b, int) or b > 0:
                    dve.wait_ge(hT_ready, b * C)
                for r in range(R):
                    last = dve.tensor_scalar(h[:, r], x_in[:, r], meanvar[:, r, 0:1], rstd[:, r:r + 1],
                                             ALU.subtract, ALU.mult)
                last.then_inc(h_made, 1)

            def mask_tile(b, u):
                t = b * TILES + u
                w = u % TILES
                r = w // GROUP % R
                dve.wait_ge(scores_ready, t + 1)
                if not isinstance(b, int) or t >= RING:
                    dve.wait_ge(probs_made, t + 1 - RING)
                dve.nop(nofuse=True)
                dve.tensor_tensor_reduce(out=masked[:, w % RING], in0=ps_scores[:, w % SCORE_BANKS],
                                         in1=mask[:, r], scale=-1.0, scalar=HUGE, op0=ALU.add,
                                         op1=ALU.min, accum_out=negmax[:, w:w + 1]).then_inc(masked_made, 1)

            def take_turned(b, u, first):
                grain = u // GROUP
                dve.wait_ge(turned, b * TILES + u + 1)
                if not first or grain >= 4:
                    dve.wait_ge(mixed, b * (GRAINS // 2) + grain // 2 - 1)
                dve.tensor_copy(probsT[:, grain % 4, DVE_TURNED], ps_turned[:, u % 2]).then_inc(turned_out_dve, 1)

            def hT_lo(b, c):
                dve.wait_ge(hT_hi_made, b * C + c + 1)
                dve.scalar_tensor_tensor(hT[:, 1, c], bank(TURN_H[c]), 0.0, hT[:, 0, c].bitcast(F32),
                                         ALU.max, ALU.subtract).then_inc(hT_lo_made, 1)

            def hi_part(b, c, i):
                dve.wait_ge(full_made, b * 4 + 2 * c + i + 1)
                if not isinstance(b, int) or b > 0:
                    dve.wait_ge(stacked[c], b * STACKED)
                dve.tensor_copy(split[:, c, 2 * i], full[:, i]).then_inc(hi_made, 1)

            def take_v(b, par, half):
                dve.wait_ge(v_ready, b * 2 + half + 1)
                dve.tensor_tensor(v[:, par, 2 * half:2 * half + 2], row_tiles(bank((V_0, V_1)[half])),
                                  bias_v[:].unsqueeze(1).to_broadcast([P, 2, D]), ALU.add).then_inc(v_made, 1)

            def invert_sums(b, par, g, fresh):
                dve.wait_ge(probs_made, b * TILES + GT * (g + 1))
                dve.reciprocal(recip[:], sums[:, par, GT * g:GT * g + GT]).then_inc(recip_made, 1)
                dve.wait_ge(recip_made, b * 2 + g + 1)
                if not fresh:
                    dve.wait_ge(recipT_ready, b * 2 + g)
                dve.tensor_copy(recip_wide[:], recip[:].rearrange("p (r j) -> p r j", j=GROUP)
                                .unsqueeze(3).to_broadcast([P, R, GROUP, HD])).then_inc(recip_spread, 1)

            def divide(b, g):
                dve.wait_ge(mixed, b * (GRAINS // 2) + 2 * g + 2)
                dve.wait_ge(recipT_made, b * 2 + g + 1)
                if not isinstance(b, int) or b > 0:
                    dve.wait_ge(attn_lo_made, b * 2 + g - 1)
                dve.tensor_tensor(attn_full[:, g], ps_mixed[:].rearrange("p r q -> p (r q)"), recipT[:],
                                  ALU.mult).then_inc(divided, 1)

            def take_y(b, par, half):
                dve.wait_ge(out_ready, b * 2 + half + 1)
                dve.wait_ge(residual_made, b + 1)
                dve.tensor_tensor(residual[:, par, 2 * half:2 * half + 2], row_tiles(bank((OUT_0, OUT_1)[half])),
                                  residual[:, par, 2 * half:2 * half + 2], ALU.add).then_inc(y_made, 1)

            def slot(b, par, first, last):
                for u in range(TILES):
                    ahead = u + MASK_AHEAD
                    if not last or ahead < TILES:
                        mask_tile(b, ahead)
                    if u % GROUP == DVE_TURNED:
                        take_turned(b, u, first)
                    for g in range(2):
                        if u == INVERT_AT[g]:
                            invert_sums(b, par, g, first and g == 0)
                    if u == DIVIDE_AT[1] and not first:
                        divide(b - 1, 1)
                    if u == DIVIDE_AT[0]:
                        divide(b, 0)
                    for half in range(2):
                        if u == OUT_AT[half][-1] + 1 and not first:
                            take_y(b - 1, 1 - par, half)
                    if not last:
                        for half in range(2):
                            if u == STATS_AT[half]:
                                statistics(b + 1, (2 * half, 2 * half + 1))
                        if u == VARIANCE_AT:
                            mean_and_variance(b + 1)
                        if u == NORMAL_AT:
                            normalise(b + 1)
                        for c in range(C):
                            if u == TURN_H_AT[c] + 2:
                                hT_lo(b + 1, c)
                            if u == Q_AT[c][-1] + 2:
                                hi_part(b + 1, c, 0)
                            if u == K_AT[c][-1] + 2:
                                hi_part(b + 1, c, 1)
                        for half in range(2):
                            if u == V_AT[half][-1] + 1:
                                take_v(b + 1, 1 - par, half)

            def split_weights(n, w, i):
                dve.wait_ge(w_loaded[n], 16)
                dve.tensor_copy(w[:, 0], w_in[:, i]).then_inc(w_hi_made, 1)
                dve.wait_ge(w_hi_made, n + 1)
                dve.tensor_tensor(w[:, 1], w_in[:, i], w[:, 0].bitcast(F32), ALU.subtract).then_inc(w_split, 1)

            statistics(0, range(R))
            mean_and_variance(0)
            split_weights(0, w_q, 0)
            normalise(0)
            split_weights(1, w_k, 1)
            hT_lo(0, 0)
            hT_lo(0, 1)
            split_weights(2, w_v, 0)
            for c in range(C):
                hi_part(0, c, 0)
                hi_part(0, c, 1)
            dve.wait_ge(bias_loaded, 80)
            for r in range(R):
                last = dve.tensor_scalar(mask[:, r].rearrange("p (k q) -> p k q", k=R),
                                         adj_in[:, r].rearrange("p (q k) -> p k q", k=R),
                                         1.0, BIG, ALU.subtract, ALU.mult)
            last.then_inc(mask_made, 1)
            take_v(0, 0, 0)
            take_v(0, 0, 1)
            split_weights(3, w_o, 1)
            dve.wait_ge(mask_made, 1)
            for u in range(MASK_AHEAD):
                mask_tile(0, u)
            slots(dve, slot)
            divide(NB - 1, 1)
            take_y(NB - 1, 1, 0)
            take_y(NB - 1, 1, 1)

        @block.tensor
        def _(pe):
            PARTS = ((0, 0), (0, 1), (1, 0))

            def scores(b, par, u):
                t = b * TILES + u
                w = u % TILES
                g, r, j = w // GT, w // GROUP % R, w % GROUP
                if r == 0 and j == 0:
                    pe.wait_ge(stacked[g], (b + u // TILES) * STACKED + STACKED)
                back = SCORE_BANKS if w >= SCORE_BANKS else w + TILES - last_in_bank(w)
                if not isinstance(b, int) or t >= back:
                    pe.wait_ge(masked_made, t + 1 - back)
                pe.matmul(ps_scores[:, w % SCORE_BANKS], stack[:, par, GROUP * g + j, 0, r * P:r * P + P],
                          stack[:, par, GROUP * g + j, 1], start=True, stop=True).then_inc(scores_ready, 1)

            def turn(b, u, first):
                t = b * TILES + u
                pe.wait_ge(probs_made, t + 1)
                if not first or u >= 2:
                    if (u - 2) % GROUP == DVE_TURNED:
                        pe.wait_ge(turned_out_dve, b * GRAINS + (u - 2) // GROUP + 1)
                    else:
                        done = (u - 2) // GROUP * 3 + (u - 2) % GROUP + ((u - 2) % GROUP < DVE_TURNED)
                        pe.wait_ge(turned_out_act, b * (TILES - GRAINS) + done)
                for k in range(R):
                    last = pe.transpose(ps_turned[:, u % 2, k], probs[:, u % RING, k * P:k * P + P], ident[:])
                last.then_inc(turned, 1)

            def mix(b, par, pair, k, first):
                g, half = pair // 2, pair % 2
                if k == 0:
                    pe.wait_ge(turned_out_act, b * (TILES - GRAINS) + 6 * pair + 6)
                    pe.wait_ge(turned_out_dve, b * GRAINS + 2 * pair + 2)
                    pe.wait_ge(v_made, b * 2 + 2)
                    if half == 0 and not (first and g == 0):
                        pe.wait_ge(divided, b * 2 + g)
                for j in range(GROUP):
                    head = GROUP * g + j
                    last = pe.matmul(ps_mixed[HD * j:HD * j + HD, 2 * half:2 * half + 2],
                                     v[:, par, k, head * HD:head * HD + HD],
                                     probsT[:, 2 * half:2 * half + 2, j, k], start=(k == 0), stop=(k == R - 1))
                if k == R - 1:
                    last.then_inc(mixed, 1)

            def turn_recip(b, g):
                pe.wait_ge(recip_spread, b * 2 + g + 1)
                place = bank((RECIP_0, RECIP_1)[g])
                for r in range(R):
                    last = pe.transpose(place[:, r * P:r * P + P],
                                        recip_wide[:, r].rearrange("p j d -> p (j d)"), ident[:])
                last.then_inc(recipT_ready, 1)

            def turn_h(b, c):
                pe.wait_ge(h_made, b + 1)
                for r in range(R):
                    last = pe.transpose(bank(TURN_H[c])[:, r * P:r * P + P], h[:, r, c * P:c * P + P], ident[:])
                last.then_inc(hT_ready, 1)

            def project_qk(b, place, w, half, part):
                h_part, w_part = PARTS[part]
                for c in range(C):
                    last = pe.matmul(bank(place), w[:, w_part, c, half * P:half * P + P], hT[:, h_part, c],
                                     start=(part == 0 and c == 0), stop=(part == 2 and c == C - 1))
                if part == 2:
                    last.then_inc(qk_ready, 1)

            def project_rows(left, w, place, half, third, done):
                for n in range(4 * third, 4 * third + 4):
                    i, part, c = n // 6, n // 2 % 3, n % 2
                    r = 2 * half + i
                    left_part, w_part = PARTS[part]
                    last = pe.matmul(bank(place)[:, i * D:i * D + D], left[:, left_part, c, r * P:r * P + P],
                                     w[:, w_part, c], start=(part == 0 and c == 0), stop=(part == 2 and c == C - 1))
                if third == 2:
                    last.then_inc(done, 1)

            def pieces_of_last(b, u, next_projected, final=False):
                if u == RECIP_AT[1]:
                    if final:
                        pe.wait_ge(y_made, b * 2)
                        pe.wait_ge(recipT_made, b * 2 + 1)
                    else:
                        pe.wait_ge(v_made, b * 2 + 3)
                    turn_recip(b, 1)
                for half in range(2):
                    for third in range(3):
                        if u == OUT_AT[half][third]:
                            if third == 0:
                                pe.wait_ge(attn_lo_made, b * 2 + 2)
                                pe.wait_ge(recipT_made, b * 2 + 2)
                                if next_projected:
                                    pe.wait_ge(full_made, b * 4 + 9 + half)
                                elif not final:
                                    pe.wait_ge(v_made, b * 2 + 4)
                            project_rows(attnT, w_o, (OUT_0, OUT_1)[half], half, third, out_ready)

            def pieces_of_next(b, u, first, loading):
                n = b * 4
                if u == TURN_H_AT[0]:
                    if not loading:
                        pe.wait_ge(v_made, b * 2)
                    turn_h(b, 0)
                if u == TURN_H_AT[1]:
                    if not loading:
                        if first:
                            pe.wait_ge(v_made, b * 2 - 1)
                        else:
                            pe.wait_ge(recipT_made, b * 2 - 2)
                    turn_h(b, 1)
                for half in range(2):
                    for part in range(3):
                        if u == Q_AT[half][part]:
                            if part == 0 and half == 0:
                                pe.wait_ge(hT_hi_made, b * C + C)
                                pe.wait_ge(hT_lo_made, b * C + 1)
                                if loading:
                                    pe.wait_ge(w_split, 1)
                            if part == 2 and half == 0:
                                pe.wait_ge(hT_lo_made, b * C + C)
                            if part == 0 and half == 1:
                                if loading:
                                    pe.wait_ge(full_made, n + 2)
                                elif first:
                                    pe.wait_ge(recipT_made, b * 2 - 1)
                                    pe.wait_ge(full_made, n + 2)
                                else:
                                    pe.wait_ge(y_made, b * 2 - 2)
                            project_qk(b, (Q_0, Q_1)[half], w_q, half, part)
                        if u == K_AT[half][part]:
                            if part == 0 and half == 0 and loading:
                                pe.wait_ge(w_split, 2)
                            if part == 0 and half == 1:
                                if loading:
                                    pe.wait_ge(full_made, n + 1)
                                else:
                                    pe.wait_ge(recipT_made, b * 2 - 1)
                            project_qk(b, (K_0, K_1)[half], w_k, half, part)
                for half in range(2):
                    for third in range(3):
                        if u == V_AT[half][third]:
                            if third == 0:
                                pe.wait_ge(full_made, n + 3 + half)
                                if loading:
                                    pe.wait_ge(w_split, 3)
                            project_rows(hT, w_v, (V_0, V_1)[half], half, third, v_ready)

            def slot(b, par, first, last):
                for u in range(TILES):
                    ahead = u + SCORES_AHEAD
                    if not last or ahead < TILES:
                        scores(b, par ^ (ahead >= TILES), ahead)
                    turn(b, u, first)
                    if u % 8 in MIX_AT:
                        pair, k = u // 8 - 1, MIX_AT.index(u % 8)
                        if pair >= 0:
                            mix(b, par, pair, k, first)
                        elif not first:
                            mix(b - 1, 1 - par, GRAINS // 2 - 1, k, False)
                    if not first:
                        pieces_of_last(b - 1, u, not last)
                    if u == RECIP_AT[0]:
                        if first:
                            pe.wait_ge(hT_lo_made, b * C + 2 * C)
                            pe.wait_ge(full_made, b * 4 + 4 + 2)
                        else:
                            pe.wait_ge(y_made, b * 2 - 1)
                        turn_recip(b, 0)
                    if not last:
                        pieces_of_next(b + 1, u, first, False)

            pe.wait_ge(ident_made, 3)
            for u in range(TILES):
                pieces_of_next(0, u, True, True)
            for u in range(SCORES_AHEAD):
                scores(0, 0, u)
            pe.wait_ge(w_split, 4)
            slots(pe, slot)
            for k in range(R):
                mix(NB - 1, 1, GRAINS // 2 - 1, k, False)
            for u in range(TILES):
                pieces_of_last(NB - 1, u, False, final=True)


_INS = ["x", "adj", "L0_gnn_Wq", "L0_gnn_bq", "L0_gnn_Wk", "L0_gnn_bk", "L0_gnn_Wv", "L0_gnn_bv",
        "L0_gnn_Wo", "L0_gnn_bo"]


def kernel(**inputs):
    import concourse.bacc as bacc
    import numpy as np
    from concourse.bass_utils import run_bass_kernel_spmd

    nc = bacc.Bacc("TRN2", target_bir_lowering=False, num_devices=1)
    arrays, args = {}, []
    for name in _INS:
        a = np.ascontiguousarray(inputs[name])
        arrays[f"in_{name}_dram"] = a
        args.append(nc.dram_tensor(f"in_{name}_dram", a.shape, mybir.dt.from_np(a.dtype), kind="ExternalInput").ap())
    shape = inputs["x"].shape
    args.append(nc.dram_tensor("out_0_dram", shape, F32, kind="ExternalOutput").ap())
    graph_attention(nc, *args)
    r = run_bass_kernel_spmd(nc, [arrays], core_ids=[0])
    return r.results[0]["out_0_dram"]
```

```python
from contextlib import ExitStack

import concourse.bass as bass
from concourse import mybir

ALU = mybir.AluOpType
ACT = mybir.ActivationFunctionType
F32 = mybir.dt.float32
F32R = mybir.dt.float32r

P = 128
HEADS = 8
GROUP = 4
PAIR = 2 * GROUP
EPS = 1e-5
BIG = 1e9
HUGE = 3.0e38
STACKING = ((0, 2), (0, 3), (1, 2), (1, 3))
STACKED = 16 * len(STACKING)
DIRECT = 4
WARMING = (9, 4)

SCORES_AHEAD = 3
MASK_AHEAD = 3
EXP_AHEAD = 2
SCORE_BANKS = 3
RING = 4
DVE_TURNED = (3, 5)
MISC = 2

RECIP_1, TURN_H, Q_0, K_0, OUT_0, OUT_1, RECIP_0, Q_1, K_1, V_0, V_1 = 0, (1, 2), 3, 4, 5, 6, 7, 8, 9, 10, 11
MIX_AT = (4, 4, 7, 7)
RECIP_AT = (20, 1)
TURN_H_AT = (3, 4)
Q_AT = ((7, 8, 9), (21, 22, 23))
K_AT = ((10, 11, 12), (24, 25, 26))
OUT_AT = ((14, 15, 16), (17, 18, 19))
V_AT = ((27, 28, 28), (29, 30, 31))
STATS_AT = (14, 16, 18, 19)
VARIANCE_AT = 21
NORMAL_AT = (0, 0, 1, 1)
INVERT_AT = (15, 31)
DIVIDE_AT = (24, 8)
ATTN_HI_AT = (26, 10)


def graph_attention(nc, x, adj, wq, bq, wk, bk, wv, bv, wo, bo, out):
    NB, N, D = x.shape
    HD = D // HEADS
    R = N // P
    C = D // P
    TILES = HEADS * R
    GT = GROUP * R
    PAIRS = TILES // PAIR
    SCALE = float(HD) ** -0.5
    assert HD == 32 and R == 4 and C == 2 and GROUP * HD == P and NB % 2 == 0

    x_rows = x.rearrange("b (p r) d -> b p r d", r=R)
    out_rows = out.rearrange("b (p r) d -> b p r d", r=R)

    with ExitStack() as ctx:
        def sb(name, shape, dt=F32):
            return ctx.enter_context(nc.sbuf_tensor(name, shape, dt))

        def psum(name, shape):
            return ctx.enter_context(nc.psum_tensor(name, shape, F32))

        def sem(name):
            return ctx.enter_context(nc.semaphore(name))

        ident = sb("ident", [P, P])
        minus_half = sb("minus_half", [P, R])
        mask = sb("mask", [P, R, N])
        w_q, w_k, w_v, w_o = (sb(n, [P, 2, C, D], F32R) for n in ("w_q", "w_k", "w_v", "w_o"))
        bias_q = sb("bias_q", [P, C])
        bias_qs = sb("bias_qs", [P, C])
        bias_k = sb("bias_k", [P, C])
        bias_v = sb("bias_v", [P, D])
        bias_o = sb("bias_o", [P, D])
        x_in = sb("x_in", [P, R, D])
        residual = sb("residual", [P, 2, R, D])
        bn = sb("bn", [P, R, 6])
        meanvar = sb("meanvar", [P, R, 2])
        variance = sb("variance", [P, R])
        rstd = sb("rstd", [P, R])
        h = sb("h", [P, R, D])
        hT = sb("hT", [P, 2, C, N], F32R)
        full = sb("full", [P, 2, N])
        split = sb("split", [P, C, 4, N], F32R)
        stack = sb("stack", [P, 2, HEADS, 2, N], F32R)
        v = sb("v", [P, 2, R, D])
        masked = sb("masked", [P, RING, N])
        negmax = sb("negmax", [P, TILES])
        probs = sb("probs", [P, RING, N])
        sums = sb("sums", [P, 2, TILES])
        probsT = sb("probsT", [P, 4, GROUP, R, P])
        adj_in = probsT[:, 3].rearrange("p j k q -> p (j k q)").rearrange("p (r n) -> p r n", r=R)
        w_in = probsT[:, 2, 0:2].rearrange("p j k q -> p (j k q)").rearrange("p (i c d) -> p i c d", i=2, c=C)
        recip = sb("recip", [P, GT])
        recip_wide = sb("recip_wide", [P, R, GROUP, HD])
        recipT = sb("recipT", [P, N])
        attn_full = sb("attn_full", [P, 2, N])
        attnT = sb("attnT", [P, 2, 2, N], F32R)

        ps_scores = psum("ps_scores", [P, SCORE_BANKS, N])
        ps_turned = psum("ps_turned", [P, 2, R, P])
        ps_mixed = psum("ps_mixed", [P, R, P])
        ps_misc = psum("ps_misc", [P, MISC, N])
        ps_end = ps_scores[:, 0, :2 * P].rearrange("p (r q) -> p r q", r=2)
        ps_out_end = (ps_misc[:, :, :D], ps_turned[:].rearrange("p i k q -> p i (k q)")[:, :, :D])

        w_loaded = [sem(f"w_loaded{i}") for i in range(4)]
        bias_loaded, w_hi_made, w_split = sem("bias_loaded"), sem("w_hi_made"), sem("w_split")
        ident_made, bias_scaled, mask_made = sem("ident_made"), sem("bias_scaled"), sem("mask_made")
        x_loaded, residual_loaded = sem("x_loaded"), sem("residual_loaded")
        bn_made, meanvar_made = sem("bn_made"), sem("meanvar_made")
        variance_made, rstd_made = sem("variance_made"), sem("rstd_made")
        h_made, residual_made = sem("h_made"), sem("residual_made")
        hT_ready, hT_hi_made, hT_lo_made = sem("hT_ready"), sem("hT_hi_made"), sem("hT_lo_made")
        qk_ready, full_made, hi_made, split_made = sem("qk_ready"), sem("full_made"), sem("hi_made"), sem("split_made")
        stacked = [sem(f"stacked{head}") for head in range(HEADS)]
        v_ready, v_made = sem("v_ready"), sem("v_made")
        scores_ready, masked_made, probs_made = sem("scores_ready"), sem("masked_made"), sem("probs_made")
        turned, turned_out_act, turned_out_dve = sem("turned"), sem("turned_out_act"), sem("turned_out_dve")
        mixed = sem("mixed")
        recip_made, recip_spread = sem("recip_made"), sem("recip_spread")
        recipT_ready, recipT_made = sem("recipT_ready"), sem("recipT_made")
        divided, attn_hi_made, attn_lo_made = sem("divided"), sem("attn_hi_made"), sem("attn_lo_made")
        attn_end_made = sem("attn_end_made")
        out_ready, y_made = sem("out_ready"), sem("y_made")
        y_stored = [sem(f"y_stored{i}") for i in range(2)]

        def bank(place):
            return ps_misc[:, place % MISC]

        def last_in_bank(w):
            return (TILES - 1 - w % SCORE_BANKS) // SCORE_BANKS * SCORE_BANKS + w % SCORE_BANKS

        def row_tiles(ap):
            return ap.rearrange("p (r d) -> p r d", r=2)

        block = ctx.enter_context(nc.Block())

        def slots(eng, slot):
            slot(0, 0, True, False)
            with eng.Fori(0, NB // 2 - 1) as i:
                slot(i * 2 + 1, 1, False, False)
                slot(i * 2 + 2, 0, False, False)
            slot(NB - 1, 1, False, True)

        def slots_with_x(eng, slot):
            slot(0, 0, True, False, True)
            with eng.Fori(0, NB // 2 - 2) as i:
                slot(i * 2 + 1, 1, False, False, True)
                slot(i * 2 + 2, 0, False, False, True)
            slot(NB - 3, 1, False, False, True)
            slot(NB - 2, 0, False, False, False)
            slot(NB - 1, 1, False, True, False)

        @block.sync
        def _(sp):
            def load_x(b):
                sp.dma_start(x_in[:], x_rows[b]).then_inc(x_loaded, 16)

            def load_x_when_free(b):
                sp.wait_ge(h_made, b)
                sp.nop(nofuse=True)
                load_x(b)

            def load_residual(b, par, fresh):
                if not fresh:
                    sp.wait_ge(y_stored[0], b * 16 - 16)
                    sp.nop(nofuse=True)
                    sp.wait_ge(y_stored[1], b * 16 - 16)
                    sp.nop(nofuse=True)
                sp.dma_start(residual[:, par], x_rows[b]).then_inc(residual_loaded, 16)

            def stack_half(b, par, c):
                sp.wait_ge(split_made, b * 4 + 2 * c + 2)
                sp.nop(nofuse=True)
                for j in range(GROUP):
                    for s, (q_part, k_part) in enumerate(STACKING):
                        src = split[HD * j:HD * j + HD, c, q_part:k_part + 1:k_part - q_part, :]
                        sp.dma_start(stack[HD * s:HD * s + HD, par, GROUP * c + j].bitcast(F32),
                                     src.bitcast(F32)).then_inc(stacked[GROUP * c + j], 16)

            def store(b, par, half):
                sp.wait_ge(y_made, b * 2 + half + 1)
                sp.nop(nofuse=True)
                sp.dma_start(out_rows[b][:, 2 * half:2 * half + 2, :],
                             residual[:, par, 2 * half:2 * half + 2, :]).then_inc(y_stored[half], 16)

            def slot(b, par, first, last, load):
                if load:
                    load_x_when_free(b + 2)
                if not last:
                    if not first:
                        sp.wait_ge(scores_ready, b * TILES)
                        sp.nop(nofuse=True)
                    stack_half(b + 1, 1 - par, 0)
                if not first:
                    store(b - 1, 1 - par, 0)
                    store(b - 1, 1 - par, 1)
                if not last:
                    load_residual(b + 1, 1 - par, first)
                    stack_half(b + 1, 1 - par, 1)

            load_x(0)
            sp.dma_start(w_in[:, 0], wq.rearrange("(c p) n -> p c n", p=P)).then_inc(w_loaded[0], 16)
            sp.dma_start(w_in[:, 1], wk.rearrange("(c p) n -> p c n", p=P)).then_inc(w_loaded[1], 16)
            for i, src in enumerate((wv, wo)):
                sp.wait_ge(w_split, i + 1)
                sp.dma_start(w_in[:, i], src.rearrange("(c p) n -> p c n", p=P)).then_inc(w_loaded[2 + i], 16)
            load_x_when_free(1)
            load_residual(0, 0, True)
            stack_half(0, 0, 0)
            stack_half(0, 0, 1)
            slots_with_x(sp, slot)
            store(NB - 1, 1, 0)
            store(NB - 1, 1, 1)
            sp.wait_ge(y_stored[0], 16 * NB)
            sp.wait_ge(y_stored[1], 16 * NB)

        @block.gpsimd
        def _(pool):
            def inverse_deviation(b):
                pool.wait_ge(meanvar_made, b * R + R)
                if not isinstance(b, int) or b > 0:
                    pool.wait_ge(h_made, b)
                pool.nop(nofuse=True)
                pool.tensor_scalar(variance[:], meanvar[:, :, 1], EPS, None, ALU.add).then_inc(variance_made, 1)
                pool.wait_ge(variance_made, b + 1)
                pool.tensor_tensor(rstd[:], variance[:], minus_half[:], ALU.pow).then_inc(rstd_made, 1)

            def add_bias(b, par):
                pool.wait_ge(residual_loaded, b * 16 + 16)
                pool.tensor_tensor(residual[:, par], residual[:, par],
                                   bias_o[:].unsqueeze(1).to_broadcast([P, R, D]), ALU.add).then_inc(residual_made, 1)

            def lo_part(b, c, i):
                pool.wait_ge(hi_made, b * 4 + 2 * c + i + 1)
                pool.tensor_tensor(split[:, c, 2 * i + 1], full[:, i], split[:, c, 2 * i].bitcast(F32),
                                   ALU.subtract).then_inc(split_made, 1)

            def attn_lo(b, g):
                pool.wait_ge(attn_hi_made, b * 2 + g + 1)
                if not isinstance(b, int) or b > 0:
                    pool.wait_ge(out_ready, b * 2)
                pool.tensor_tensor(attnT[:, 1, g], attn_full[:, g], attnT[:, 0, g].bitcast(F32),
                                   ALU.subtract).then_inc(attn_lo_made, 1)

            def slot(b, par, first, last, load):
                if not first:
                    attn_lo(b - 1, 1)
                if not last:
                    lo_part(b + 1, 0, 0)
                    lo_part(b + 1, 0, 1)
                if load:
                    inverse_deviation(b + 2)
                attn_lo(b, 0)
                if not last:
                    add_bias(b + 1, 1 - par)
                    lo_part(b + 1, 1, 0)
                    lo_part(b + 1, 1, 1)

            pool.memset(ident[:], 0.0).then_inc(ident_made, 1)
            pool.memset(minus_half[:], -0.5).then_inc(ident_made, 1)
            pool.wait_ge(ident_made, 2)
            pool.affine_select(out=ident[:], in_=ident[:], compare_op=ALU.not_equal, fill=1.0, base=0,
                               pattern=[[-1, P]], channel_multiplier=1).then_inc(ident_made, 1)
            inverse_deviation(0)
            pool.wait_ge(bias_loaded, 80)
            pool.tensor_scalar(bias_qs[:], bias_q[:], SCALE, None, ALU.mult).then_inc(bias_scaled, 1)
            inverse_deviation(1)
            add_bias(0, 0)
            slots_with_x(pool, slot)

        @block.scalar
        def _(act):
            def exponentials(b, par, u):
                t = b * TILES + u
                w = u % TILES
                act.wait_ge(masked_made, t + 1)
                if not isinstance(b, int) or t >= RING:
                    act.wait_ge(turned, t + 1 - RING)
                act.activation(probs[:, w % RING], masked[:, w % RING], ACT.Exp, scale=-1.0,
                               bias=negmax[:, w:w + 1],
                               accum_out=sums[:, par, w:w + 1]).then_inc(probs_made, 1)

            def take_turned(b, u, first):
                grain, j = u // GROUP, u % GROUP
                act.wait_ge(turned, b * TILES + u + 1)
                if not first or grain >= 4:
                    act.wait_ge(mixed, b * PAIRS + grain // 2 - 1)
                act.copy(probsT[:, grain % 4, j], ps_turned[:, u % 2]).then_inc(turned_out_act, 1)

            def hT_hi(b, c):
                act.wait_ge(hT_ready, b * C + c + 1)
                act.activation(hT[:, 0, c], bank(TURN_H[c]), ACT.Relu).then_inc(hT_hi_made, 1)

            def take_qk(b, c, i, fresh):
                act.wait_ge(qk_ready, b * 4 + 2 * c + i + 1)
                if not fresh:
                    act.wait_ge(split_made, b * 4 + 2 * c + i - 1)
                if i == 0:
                    act.activation(full[:, 0], bank((Q_0, Q_1)[c]), ACT.Identity, scale=SCALE,
                                   bias=bias_qs[:, c:c + 1]).then_inc(full_made, 1)
                else:
                    act.activation(full[:, 1], bank((K_0, K_1)[c]), ACT.Identity,
                                   bias=bias_k[:, c:c + 1]).then_inc(full_made, 1)

            def take_recipT(b, g, fresh):
                act.wait_ge(recipT_ready, b * 2 + g + 1)
                if not fresh:
                    act.wait_ge(divided, b * 2 + g)
                act.copy(recipT[:], bank((RECIP_0, RECIP_1)[g])).then_inc(recipT_made, 1)

            def slot(b, par, first, last):
                for u in range(TILES):
                    ahead = u + EXP_AHEAD
                    if not last or ahead < TILES:
                        exponentials(b, par ^ (ahead >= TILES), ahead)
                    if u % PAIR not in DVE_TURNED:
                        take_turned(b, u, first)
                    if not first:
                        if u == RECIP_AT[1] + 1:
                            take_recipT(b - 1, 1, False)
                    if u == RECIP_AT[0] + 1:
                        take_recipT(b, 0, first)
                    if not last:
                        for c in range(C):
                            if u == TURN_H_AT[c] + 1:
                                hT_hi(b + 1, c)
                            if u == Q_AT[c][-1] + 1:
                                take_qk(b + 1, c, 0, False)
                            if u == K_AT[c][-1] + 1:
                                take_qk(b + 1, c, 1, False)

            act.dma_start(bias_q[:], bq.rearrange("(c p) -> p c", p=P),
                          allow_slow_non_contiguous=True).then_inc(bias_loaded, 16)
            act.dma_start(bias_k[:], bk.rearrange("(c p) -> p c", p=P),
                          allow_slow_non_contiguous=True).then_inc(bias_loaded, 16)
            act.dma_start(bias_v[:], bv.unsqueeze(0).to_broadcast([P, D])).then_inc(bias_loaded, 16)
            act.dma_start(bias_o[:], bo.unsqueeze(0).to_broadcast([P, D])).then_inc(bias_loaded, 16)
            act.dma_start(adj_in[:], adj.rearrange("(p r) k -> p r k", r=R)).then_inc(bias_loaded, 16)
            hT_hi(0, 0)
            hT_hi(0, 1)
            act.wait_ge(bias_scaled, 1)
            act.wait_ge(bias_loaded, 80)
            for c in range(C):
                take_qk(0, c, 0, c == 0)
                take_qk(0, c, 1, c == 0)
            for u in range(EXP_AHEAD):
                exponentials(0, 0, u)
            slots(act, slot)
            take_recipT(NB - 1, 1, False)
            for half in range(2):
                cols = slice(half * 2 * P, half * 2 * P + 2 * P)
                act.wait_ge(divided, NB * 2 + half)
                act.copy(attnT[:, 0, 1, cols], attn_full[:, 1, cols]).then_inc(attn_hi_made, 1)

        @block.vector
        def _(dve):
            def statistics(b, rows):
                if rows[0] == 0:
                    dve.wait_ge(x_loaded, b * 16 + 16)
                for r in rows:
                    dve.bn_stats(bn[:, r], x_in[:, r]).then_inc(bn_made, 1)

            def mean_and_variance(b):
                dve.wait_ge(bn_made, b * R + R)
                if not isinstance(b, int) or b > 0:
                    dve.wait_ge(variance_made, b)
                dve.nop(nofuse=True)
                for r in range(R):
                    dve.bn_aggr(meanvar[:, r], bn[:, r]).then_inc(meanvar_made, 1)

            def normalise(b, rows):
                if rows[0] == 0:
                    dve.wait_ge(meanvar_made, b * R + R)
                    dve.wait_ge(rstd_made, b + 1)
                    if not isinstance(b, int) or b > 0:
                        dve.wait_ge(hT_ready, b * C)
                for r in rows:
                    last = dve.tensor_scalar(h[:, r], x_in[:, r], meanvar[:, r, 0:1], rstd[:, r:r + 1],
                                             ALU.subtract, ALU.mult)
                if rows[-1] == R - 1:
                    last.then_inc(h_made, 1)

            def mask_tile(b, u):
                t = b * TILES + u
                w = u % TILES
                r = w // GROUP % R
                dve.wait_ge(scores_ready, t + 1)
                if not isinstance(b, int) or t >= RING:
                    dve.wait_ge(probs_made, t + 1 - RING)
                dve.nop(nofuse=True)
                dve.tensor_tensor_reduce(out=masked[:, w % RING], in0=ps_scores[:, w % SCORE_BANKS],
                                         in1=mask[:, r], scale=-1.0, scalar=HUGE, op0=ALU.add,
                                         op1=ALU.min, accum_out=negmax[:, w:w + 1]).then_inc(masked_made, 1)

            def take_turned(b, u, first):
                grain, j = u // GROUP, u % GROUP
                dve.wait_ge(turned, b * TILES + u + 1)
                if not first or grain >= 4:
                    dve.wait_ge(mixed, b * PAIRS + grain // 2 - 1)
                dve.tensor_copy(probsT[:, grain % 4, j], ps_turned[:, u % 2]).then_inc(turned_out_dve, 1)

            def hT_lo(b, c):
                dve.wait_ge(hT_hi_made, b * C + c + 1)
                dve.scalar_tensor_tensor(hT[:, 1, c], bank(TURN_H[c]), 0.0, hT[:, 0, c].bitcast(F32),
                                         ALU.max, ALU.subtract).then_inc(hT_lo_made, 1)

            def hi_part(b, c, i):
                dve.wait_ge(full_made, b * 4 + 2 * c + i + 1)
                if not isinstance(b, int) or b > 0:
                    for j in range(GROUP):
                        dve.wait_ge(stacked[GROUP * c + j], b * STACKED)
                dve.tensor_copy(split[:, c, 2 * i], full[:, i]).then_inc(hi_made, 1)

            def take_v(b, par, half):
                dve.wait_ge(v_ready, b * 2 + half + 1)
                dve.tensor_tensor(v[:, par, 2 * half:2 * half + 2], row_tiles(bank((V_0, V_1)[half])),
                                  bias_v[:].unsqueeze(1).to_broadcast([P, 2, D]), ALU.add).then_inc(v_made, 1)

            def invert_sums(b, par, g, fresh):
                dve.wait_ge(probs_made, b * TILES + GT * (g + 1))
                dve.reciprocal(recip[:], sums[:, par, GT * g:GT * g + GT]).then_inc(recip_made, 1)
                dve.wait_ge(recip_made, b * 2 + g + 1)
                if not fresh:
                    dve.wait_ge(recipT_ready, b * 2 + g)
                dve.tensor_copy(recip_wide[:], recip[:].rearrange("p (r j) -> p r j", j=GROUP)
                                .unsqueeze(3).to_broadcast([P, R, GROUP, HD])).then_inc(recip_spread, 1)

            def divide(b, g):
                dve.wait_ge(mixed, b * PAIRS + 2 * g + 2)
                dve.wait_ge(recipT_made, b * 2 + g + 1)
                if not isinstance(b, int) or b > 0:
                    dve.wait_ge(attn_lo_made, b * 2 + g - 1)
                dve.tensor_tensor(attn_full[:, g], ps_mixed[:].rearrange("p r q -> p (r q)"), recipT[:],
                                  ALU.mult).then_inc(divided, 1)

            def attn_hi(b, g):
                dve.wait_ge(divided, b * 2 + g + 1)
                if not isinstance(b, int) or b > 0:
                    dve.wait_ge(out_ready, b * 2)
                dve.tensor_copy(attnT[:, 0, g], attn_full[:, g]).then_inc(attn_hi_made, 1)

            def take_y(b, par, half):
                dve.wait_ge(out_ready, b * 2 + half + 1)
                dve.wait_ge(residual_made, b + 1)
                dve.tensor_tensor(residual[:, par, 2 * half:2 * half + 2], row_tiles(bank((OUT_0, OUT_1)[half])),
                                  residual[:, par, 2 * half:2 * half + 2], ALU.add).then_inc(y_made, 1)

            def slot(b, par, first, last, load):
                for u in range(TILES):
                    ahead = u + MASK_AHEAD
                    if not last or ahead < TILES:
                        mask_tile(b, ahead)
                    if u % PAIR in DVE_TURNED:
                        take_turned(b, u, first)
                    for g in range(2):
                        if u == INVERT_AT[g]:
                            invert_sums(b, par, g, first and g == 0)
                    if u == DIVIDE_AT[1] and not first:
                        divide(b - 1, 1)
                    if u == ATTN_HI_AT[1] and not first:
                        attn_hi(b - 1, 1)
                    if u == ATTN_HI_AT[0]:
                        attn_hi(b, 0)
                    if u == DIVIDE_AT[0]:
                        divide(b, 0)
                    for half in range(2):
                        if u == OUT_AT[half][-1] + 1 and not first:
                            take_y(b - 1, 1 - par, half)
                    if load:
                        for r in range(R):
                            if u == STATS_AT[r]:
                                statistics(b + 2, (r,))
                        if u == VARIANCE_AT:
                            mean_and_variance(b + 2)
                    if not last:
                        for r in range(R):
                            if u == NORMAL_AT[r]:
                                normalise(b + 1, (r,))
                        for c in range(C):
                            if u == TURN_H_AT[c] + 2:
                                hT_lo(b + 1, c)
                            if u == Q_AT[c][-1] + 2:
                                hi_part(b + 1, c, 0)
                            if u == K_AT[c][-1] + 2:
                                hi_part(b + 1, c, 1)
                        for half in range(2):
                            if u == min(V_AT[half][-1] + 1, TILES - 1):
                                take_v(b + 1, 1 - par, half)

            def split_weights(n, w, i):
                dve.wait_ge(w_loaded[n], 16)
                dve.tensor_copy(w[:, 0], w_in[:, i]).then_inc(w_hi_made, 1)
                dve.wait_ge(w_hi_made, n + 1)
                dve.tensor_tensor(w[:, 1], w_in[:, i], w[:, 0].bitcast(F32), ALU.subtract).then_inc(w_split, 1)

            statistics(0, range(R))
            mean_and_variance(0)
            split_weights(0, w_q, 0)
            normalise(0, range(R))
            split_weights(1, w_k, 1)
            hT_lo(0, 0)
            hT_lo(0, 1)
            split_weights(2, w_v, 0)
            dve.wait_ge(bias_loaded, 80)
            for r in range(R):
                last = dve.tensor_scalar(mask[:, r].rearrange("p (k q) -> p k q", k=R),
                                         adj_in[:, r].rearrange("p (q k) -> p k q", k=R),
                                         1.0, BIG, ALU.subtract, ALU.mult)
            last.then_inc(mask_made, 1)
            for c in range(C):
                for i in range(2):
                    hi_part(0, c, i)
                    dve.wait_ge(hi_made, 2 * c + i + 1)
                    dve.tensor_tensor(split[:, c, 2 * i + 1], full[:, i], split[:, c, 2 * i].bitcast(F32),
                                      ALU.subtract).then_inc(split_made, 1)
                if c == 0:
                    statistics(1, range(R))
                    mean_and_variance(1)
            dve.wait_ge(mask_made, 1)
            mask_tile(0, 0)
            take_v(0, 0, 0)
            take_v(0, 0, 1)
            for u in range(1, MASK_AHEAD):
                mask_tile(0, u)
            split_weights(3, w_o, 1)
            slots_with_x(dve, slot)
            dve.wait_ge(recipT_made, NB * 2)
            dve.wait_ge(out_ready, NB * 2 - 2)
            for half in range(2):
                cols = slice(half * 2 * P, half * 2 * P + 2 * P)
                dve.wait_ge(mixed, NB * PAIRS - 1 + half)
                dve.tensor_tensor(attn_full[:, 1, cols], (ps_mixed[:, 0:2], ps_end)[half]
                                  .rearrange("p r q -> p (r q)"), recipT[:, cols], ALU.mult).then_inc(divided, 1)
                dve.wait_ge(attn_hi_made, NB * 2 + half)
                dve.tensor_tensor(attnT[:, 1, 1, cols], attn_full[:, 1, cols], attnT[:, 0, 1, cols].bitcast(F32),
                                  ALU.subtract).then_inc(attn_end_made, 1)
            for half in range(2):
                dve.wait_ge(out_ready, NB * 2 - 1 + half)
                dve.tensor_tensor(residual[:, 1, 2 * half:2 * half + 2], ps_out_end[half],
                                  residual[:, 1, 2 * half:2 * half + 2], ALU.add).then_inc(y_made, 1)

        @block.tensor
        def _(pe):
            PARTS = ((0, 0), (0, 1), (1, 0))

            def scores(b, par, u):
                t = b * TILES + u
                w = u % TILES
                g, r, j = w // GT, w // GROUP % R, w % GROUP
                direct = isinstance(b, int) and t < DIRECT
                first_stacked = r == 0
                if isinstance(b, int) and t < GT:
                    first_stacked = DIRECT <= t < DIRECT + GROUP
                if first_stacked:
                    pe.wait_ge(stacked[GROUP * g + j], (b + u // TILES) * STACKED + STACKED)
                back = SCORE_BANKS if w >= SCORE_BANKS else w + TILES - last_in_bank(w)
                if not isinstance(b, int) or t >= back:
                    pe.wait_ge(masked_made, t + 1 - back)
                if direct:
                    if t == 0:
                        pe.wait_ge(split_made, 2)
                    rows = slice(HD * j, HD * j + HD)
                    for q_part, k_part in STACKING:
                        last = pe.matmul(ps_scores[:, w % SCORE_BANKS], split[rows, g, q_part, r * P:r * P + P],
                                         split[rows, g, k_part], start=(q_part, k_part) == STACKING[0],
                                         stop=(q_part, k_part) == STACKING[-1])
                    last.then_inc(scores_ready, 1)
                    return
                pe.matmul(ps_scores[:, w % SCORE_BANKS], stack[:, par, GROUP * g + j, 0, r * P:r * P + P],
                          stack[:, par, GROUP * g + j, 1], start=True, stop=True).then_inc(scores_ready, 1)

            def wait_turned_out(b, u, by_dve):
                mine = [(w in DVE_TURNED) == by_dve for w in range(PAIR)]
                count = (b * PAIRS + u // PAIR) * sum(mine) + sum(mine[:u % PAIR + 1])
                pe.wait_ge(turned_out_dve if by_dve else turned_out_act, count)

            def turn(b, u, first):
                t = b * TILES + u
                pe.wait_ge(probs_made, t + 1)
                if not first or u >= 2:
                    wait_turned_out(b, u - 2, (u - 2) % PAIR in DVE_TURNED)
                for k in range(R):
                    last = pe.transpose(ps_turned[:, u % 2, k], probs[:, u % RING, k * P:k * P + P], ident[:])
                last.then_inc(turned, 1)

            def mix(b, par, pair, k, first, end=False):
                g, half = pair // 2, pair % 2
                place = ps_end if end else ps_mixed[:, 2 * half:2 * half + 2]
                if k == 0:
                    wait_turned_out(b, PAIR * pair + PAIR - 1, False)
                    wait_turned_out(b, PAIR * pair + PAIR - 1, True)
                    pe.wait_ge(v_made, b * 2 + 2)
                    if half == 0 and not (first and g == 0):
                        pe.wait_ge(divided, b * 2 + g)
                for j in range(GROUP):
                    head = GROUP * g + j
                    last = pe.matmul(place[HD * j:HD * j + HD], v[:, par, k, head * HD:head * HD + HD],
                                     probsT[:, 2 * half:2 * half + 2, j, k], start=(k == 0), stop=(k == R - 1))
                if k == R - 1:
                    last.then_inc(mixed, 1)

            def turn_recip(b, g):
                pe.wait_ge(recip_spread, b * 2 + g + 1)
                place = bank((RECIP_0, RECIP_1)[g])
                for r in range(R):
                    last = pe.transpose(place[:, r * P:r * P + P],
                                        recip_wide[:, r].rearrange("p j d -> p (j d)"), ident[:])
                last.then_inc(recipT_ready, 1)

            def turn_h(b, c):
                pe.wait_ge(h_made, b + 1)
                for r in range(R):
                    last = pe.transpose(bank(TURN_H[c])[:, r * P:r * P + P], h[:, r, c * P:c * P + P], ident[:])
                last.then_inc(hT_ready, 1)

            def project_qk(b, place, w, half, part):
                h_part, w_part = PARTS[part]
                for c in range(C):
                    last = pe.matmul(bank(place), w[:, w_part, c, half * P:half * P + P], hT[:, h_part, c],
                                     start=(part == 0 and c == 0), stop=(part == 2 and c == C - 1))
                if part == 2:
                    last.then_inc(qk_ready, 1)

            def project_rows(left, w, place, half, third, done):
                for n in range(4 * third, 4 * third + 4):
                    i, part, c = n // 6, n // 2 % 3, n % 2
                    r = 2 * half + i
                    left_part, w_part = PARTS[part]
                    last = pe.matmul(bank(place)[:, i * D:i * D + D], left[:, left_part, c, r * P:r * P + P],
                                     w[:, w_part, c], start=(part == 0 and c == 0), stop=(part == 2 and c == C - 1))
                if third == 2:
                    last.then_inc(done, 1)

            def pieces_of_last(b, u, next_projected):
                if u == RECIP_AT[1]:
                    pe.wait_ge(v_made, b * 2 + 3)
                    turn_recip(b, 1)
                for half in range(2):
                    for third in range(3):
                        if u == OUT_AT[half][third]:
                            if third == 0:
                                pe.wait_ge(w_split, 4)
                                pe.wait_ge(attn_lo_made, b * 2 + 2)
                                pe.wait_ge(recipT_made, b * 2 + 2)
                                if next_projected:
                                    pe.wait_ge(full_made, b * 4 + 9 + half)
                                else:
                                    pe.wait_ge(v_made, b * 2 + 4)
                            project_rows(attnT, w_o, (OUT_0, OUT_1)[half], half, third, out_ready)

            def pieces_of_next(b, u, first, loading):
                n = b * 4
                if u == TURN_H_AT[0]:
                    if not loading:
                        pe.wait_ge(v_made, b * 2)
                    turn_h(b, 0)
                if u == TURN_H_AT[1]:
                    if not loading:
                        if first:
                            pe.wait_ge(v_made, b * 2 - 1)
                        else:
                            pe.wait_ge(recipT_made, b * 2 - 2)
                    turn_h(b, 1)
                for half in range(2):
                    for part in range(3):
                        if u == Q_AT[half][part]:
                            if part == 0 and half == 0:
                                pe.wait_ge(hT_hi_made, b * C + C)
                                pe.wait_ge(hT_lo_made, b * C + 1)
                                if loading:
                                    pe.wait_ge(w_split, 1)
                            if part == 2 and half == 0:
                                pe.wait_ge(hT_lo_made, b * C + C)
                            if part == 0 and half == 1:
                                if loading:
                                    pe.wait_ge(full_made, n + 2)
                                elif first:
                                    pe.wait_ge(recipT_made, b * 2 - 1)
                                    pe.wait_ge(full_made, n + 2)
                                else:
                                    pe.wait_ge(y_made, b * 2 - 2)
                            project_qk(b, (Q_0, Q_1)[half], w_q, half, part)
                        if u == K_AT[half][part]:
                            if part == 0 and half == 0 and loading:
                                pe.wait_ge(w_split, 2)
                            if part == 0 and half == 1:
                                if loading:
                                    pe.wait_ge(full_made, n + 1)
                                else:
                                    pe.wait_ge(recipT_made, b * 2 - 1)
                            project_qk(b, (K_0, K_1)[half], w_k, half, part)
                for half in range(2):
                    for third in range(3):
                        if u == V_AT[half][third]:
                            if third == 0:
                                pe.wait_ge(full_made, n + 3 + half)
                                if loading:
                                    pe.wait_ge(w_split, 3)
                            project_rows(hT, w_v, (V_0, V_1)[half], half, third, v_ready)

            def slot(b, par, first, last):
                for u in range(TILES):
                    ahead = u + SCORES_AHEAD
                    if not last or ahead < TILES:
                        scores(b, par ^ (ahead >= TILES), ahead)
                    for k in range(R):
                        if u % PAIR == MIX_AT[k]:
                            if u >= PAIR:
                                mix(b, par, u // PAIR - 1, k, first)
                            elif not first:
                                mix(b - 1, 1 - par, PAIRS - 1, k, False)
                    turn(b, u, first)
                    if not first:
                        pieces_of_last(b - 1, u, not last)
                    if u == RECIP_AT[0]:
                        if first:
                            pe.wait_ge(hT_lo_made, b * C + 2 * C)
                            pe.wait_ge(full_made, b * 4 + 4 + 2)
                        else:
                            pe.wait_ge(y_made, b * 2 - 1)
                        turn_recip(b, 0)
                    if not last:
                        pieces_of_next(b + 1, u, first, False)

            def keep_warm(rounds):
                with pe.Fori(0, rounds) as _:
                    for _ in range(4):
                        pe.transpose(ps_scores[:, 0, :P], ident[:], ident[:])

            pe.wait_ge(ident_made, 3)
            keep_warm(WARMING[0])
            for u in range(TILES):
                if u == Q_AT[0][0]:
                    keep_warm(WARMING[1])
                if u == V_AT[0][0]:
                    scores(0, 0, 0)
                pieces_of_next(0, u, True, True)
            for u in range(1, SCORES_AHEAD):
                scores(0, 0, u)
            slots(pe, slot)
            pe.wait_ge(y_made, NB * 2 - 2)
            turn_recip(NB - 1, 1)
            pe.wait_ge(masked_made, NB * TILES)
            for k in range(R):
                mix(NB - 1, 1, PAIRS - 1, k, False, end=True)
            pe.wait_ge(attn_lo_made, NB * 2 - 1)
            pe.wait_ge(recipT_made, NB * 2)
            for c in range(C):
                for half in range(2):
                    if c == 1:
                        pe.wait_ge(attn_end_made, half + 1)
                    for part, (left_part, w_part) in enumerate(PARTS):
                        for i in range(2):
                            r = 2 * half + i
                            last = pe.matmul(ps_out_end[half][:, i],
                                             attnT[:, left_part, c, r * P:r * P + P], w_o[:, w_part, c],
                                             start=(c == 0 and part == 0), stop=(c == 1 and part == 2))
                    if c == 1:
                            last.then_inc(out_ready, 1)


_INS = ["x", "adj", "L0_gnn_Wq", "L0_gnn_bq", "L0_gnn_Wk", "L0_gnn_bk", "L0_gnn_Wv", "L0_gnn_bv",
        "L0_gnn_Wo", "L0_gnn_bo"]


def kernel(**inputs):
    import concourse.bacc as bacc
    import numpy as np
    from concourse.bass_utils import run_bass_kernel_spmd

    nc = bacc.Bacc("TRN2", target_bir_lowering=False, num_devices=1)
    arrays, args = {}, []
    for name in _INS:
        a = np.ascontiguousarray(inputs[name])
        arrays[f"in_{name}_dram"] = a
        args.append(nc.dram_tensor(f"in_{name}_dram", a.shape, mybir.dt.from_np(a.dtype), kind="ExternalInput").ap())
    shape = inputs["x"].shape
    args.append(nc.dram_tensor("out_0_dram", shape, F32, kind="ExternalOutput").ap())
    graph_attention(nc, *args)
    r = run_bass_kernel_spmd(nc, [arrays], core_ids=[0])
    return r.results[0]["out_0_dram"]
```
